# Optimizing a Trainium2 kernel written in Bass

```python
import numpy as np
import jax
import jax.numpy as jnp

def _softmax(x, axis=-1):
    return jax.nn.softmax(x, axis=axis)

def _gelu(x):
    return jax.nn.gelu(x, approximate=True)

def _silu(x):
    return jax.nn.silu(x)

def _sigmoid(x):
    return jax.nn.sigmoid(x)

def _layernorm(x, axis=-1, eps=1e-05):
    m = jnp.mean(x, axis=axis, keepdims=True)
    v = jnp.var(x, axis=axis, keepdims=True)
    return (x - m) / jnp.sqrt(v + eps)

def _scatter_add(tgt, idx, src, axis=0):
    return tgt.at[idx].add(src)

def _segment_sum(src, seg, n):
    return jax.ops.segment_sum(src, seg, n)
kernel_name = 'mk_flamingo_gated_d1_seqx_r4_439fe1'

def setup_inputs(seed: int=0):
    np.random.seed(seed)
    _w = jnp.asarray

    def _rec_inputs():
        import jax
        import jax.numpy as jnp
        _rk = jax.random.key(seed)
        x = -0.0002928 + 1 * jax.random.normal(jax.random.fold_in(_rk, 1), (8, 256, 512), jnp.float32)
        _lenS = 256 - jax.random.randint(jax.random.fold_in(_rk, 7), (8,), 0, max(1, 256 // 4) + 1, jnp.int32)
        _lenS2 = 256 - jax.random.randint(jax.random.fold_in(_rk, 8), (8,), 0, max(1, 256 // 4) + 1, jnp.int32)
        _ctx_2048P = jax.random.normal(jax.random.fold_in(_rk, 11), (8, 16, 512), jnp.float32)
        _ctx_2048c = jax.random.dirichlet(jax.random.fold_in(_rk, 511), 0.3 * jnp.ones((16,), jnp.float32), (8, 256))
        _ctx_2048t = jnp.einsum('bsk,bkd->bsd', _ctx_2048c, _ctx_2048P)
        _ctx_2048t = _ctx_2048t * jax.lax.rsqrt(jnp.mean(jnp.square(_ctx_2048t)) + 1e-12) * 0.953939
        ctx_2048 = -1.39393e-06 + 0.999914 * (_ctx_2048t + 0.3 * jax.random.normal(jax.random.fold_in(_rk, 611), (8, 256, 512), jnp.float32))
        _g = jax.random.normal(jax.random.fold_in(_rk, 9001), (2, 1), jnp.float32)
        _g = jnp.sign(_g) * jnp.maximum(jnp.abs(_g), 1.0) + (_g == 0) * 1.0
        g_xattn = _g[0]
        g_ffn = _g[1]
        return (x, ctx_2048, g_xattn, g_ffn)
    x, ctx_2048, g_xattn, g_ffn = _rec_inputs()

    def _L0_xattn_setup():
        import jax, jax.numpy as jnp
        import numpy as np
        HID = 512
        H = 32
        HK = 8
        G = H // HK
        D = HID // H
        T = 256
        W_ATT = 64
        W_SSM = 64

        def _heads(x, n):
            B, Tt, _ = x.shape
            return x.reshape(B, Tt, n, D).transpose(0, 2, 1, 3)

        def _attend(q, k, v):
            pos = jnp.arange(T)
            rel = pos[None, :] - pos[:, None]
            slopes = jnp.power(2.0, -8.0 * jnp.arange(H, dtype=jnp.float32) / H)
            alibi = slopes[:, None, None] * rel.astype(jnp.float32)
            bias = jnp.concatenate([alibi, alibi], axis=-1)
            delta = -rel
            ssm_mask = (delta >= 0) & (delta < W_SSM)
            att_mask = (delta >= 0) & (delta < W_ATT)
            mask = jnp.concatenate([ssm_mask, att_mask], axis=-1)
            scores = jnp.einsum('bhqd,bhkd->bhqk', q, k) / np.sqrt(D).astype(np.float32)
            scores = scores + bias[None]
            scores = jnp.where(mask[None, None], scores, -jnp.inf)
            wei = jax.nn.softmax(scores, axis=-1)
            return jnp.einsum('bhqk,bhkd->bhqd', wei, v)
        key = jax.random.key(seed)
        ks = jax.random.split(key, 8)
        s = lambda fan_in: 1.0 / np.sqrt(fan_in)
        return {'hidden_states': jax.random.normal(ks[0], (2, T, HID), jnp.float32), 'ssm_states': jax.random.normal(ks[1], (2, T, HID), jnp.float32), 'Wq': jax.random.normal(ks[2], (2 * HID, HID), jnp.float32) * s(2 * HID), 'Wk': jax.random.normal(ks[3], (HID, HK * D), jnp.float32) * s(HID), 'Wv': jax.random.normal(ks[4], (HID, HK * D), jnp.float32) * s(HID), 'Wsk': jax.random.normal(ks[5], (HID, HK * D), jnp.float32) * s(HID), 'Wsv': jax.random.normal(ks[6], (HID, HK * D), jnp.float32) * s(HID), 'Wo': jax.random.normal(ks[7], (HID, HID), jnp.float32) * s(HID)}
    _L0_xattn_all = _L0_xattn_setup()
    _L0_xattn_in = {k: v for k, v in _L0_xattn_all.items() if k in ('Wq', 'Wk', 'Wv', 'Wsk', 'Wsv', 'Wo')}
    del _L0_xattn_all

    def _L0_ffn_setup():
        import jax, jax.numpy as jnp
        import numpy as np
        H = 512
        I = 256
        K = 8
        E = 128
        TOPK = 4
        EPS = 1e-08
        key = jax.random.key(seed)
        ks = jax.random.split(key, 10)
        s = 0.02
        return {'x': jax.random.normal(ks[0], (4, 512, H), jnp.float32), 'w_router': jax.random.normal(ks[1], (H, E), jnp.float32) * s, 'w_gate': jax.random.normal(ks[2], (H, K * I), jnp.float32) * s, 'w_up': jax.random.normal(ks[3], (H, K * I), jnp.float32) * s, 'w_down': jax.random.normal(ks[4], (I, H), jnp.float32) * s, 'amplitudes': jax.random.normal(ks[5], (E, K, 2), jnp.float32) * 0.1, 'expert_scale': jnp.ones((E,), jnp.float32), 'shared_w_gate': jax.random.normal(ks[6], (H, 2 * I), jnp.float32) * s, 'shared_w_up': jax.random.normal(ks[7], (H, 2 * I), jnp.float32) * s, 'shared_w_down': jax.random.normal(ks[8], (2 * I, H), jnp.float32) * s}
    _L0_ffn_all = _L0_ffn_setup()
    _L0_ffn_in = {k: v for k, v in _L0_ffn_all.items() if k in ('w_router', 'w_gate', 'w_up', 'w_down', 'amplitudes', 'expert_scale', 'shared_w_gate', 'shared_w_up', 'shared_w_down')}
    del _L0_ffn_all
    return {'x': x, 'ctx_2048': ctx_2048, 'g_xattn': g_xattn, 'g_ffn': g_ffn, 'L0_xattn_Wq': _L0_xattn_in['Wq'], 'L0_xattn_Wk': _L0_xattn_in['Wk'], 'L0_xattn_Wv': _L0_xattn_in['Wv'], 'L0_xattn_Wsk': _L0_xattn_in['Wsk'], 'L0_xattn_Wsv': _L0_xattn_in['Wsv'], 'L0_xattn_Wo': _L0_xattn_in['Wo'], 'L0_ffn_w_router': _L0_ffn_in['w_router'], 'L0_ffn_w_gate': _L0_ffn_in['w_gate'], 'L0_ffn_w_up': _L0_ffn_in['w_up'], 'L0_ffn_w_down': _L0_ffn_in['w_down'], 'L0_ffn_amplitudes': _L0_ffn_in['amplitudes'], 'L0_ffn_expert_scale': _L0_ffn_in['expert_scale'], 'L0_ffn_shared_w_gate': _L0_ffn_in['shared_w_gate'], 'L0_ffn_shared_w_up': _L0_ffn_in['shared_w_up'], 'L0_ffn_shared_w_down': _L0_ffn_in['shared_w_down']}

def reference(x, ctx_2048, g_xattn, g_ffn, L0_xattn_Wq, L0_xattn_Wk, L0_xattn_Wv, L0_xattn_Wsk, L0_xattn_Wsv, L0_xattn_Wo, L0_ffn_w_router, L0_ffn_w_gate, L0_ffn_w_up, L0_ffn_w_down, L0_ffn_amplitudes, L0_ffn_expert_scale, L0_ffn_shared_w_gate, L0_ffn_shared_w_up, L0_ffn_shared_w_down):
    import jax
    import jax.numpy as jnp

    def _L0_xattn_ref(hidden_states, ssm_states, Wq, Wk, Wv, Wsk, Wsv, Wo):
        import jax, jax.numpy as jnp
        import numpy as np
        HID = 512
        H = 32
        HK = 8
        G = H // HK
        D = HID // H
        T = 256
        W_ATT = 64
        W_SSM = 64

        def _heads(x, n):
            B, Tt, _ = x.shape
            return x.reshape(B, Tt, n, D).transpose(0, 2, 1, 3)

        def _attend(q, k, v):
            pos = jnp.arange(T)
            rel = pos[None, :] - pos[:, None]
            slopes = jnp.power(2.0, -8.0 * jnp.arange(H, dtype=jnp.float32) / H)
            alibi = slopes[:, None, None] * rel.astype(jnp.float32)
            bias = jnp.concatenate([alibi, alibi], axis=-1)
            delta = -rel
            ssm_mask = (delta >= 0) & (delta < W_SSM)
            att_mask = (delta >= 0) & (delta < W_ATT)
            mask = jnp.concatenate([ssm_mask, att_mask], axis=-1)
            scores = jnp.einsum('bhqd,bhkd->bhqk', q, k) / np.sqrt(D).astype(np.float32)
            scores = scores + bias[None]
            scores = jnp.where(mask[None, None], scores, -jnp.inf)
            wei = jax.nn.softmax(scores, axis=-1)
            return jnp.einsum('bhqk,bhkd->bhqd', wei, v)
        B = hidden_states.shape[0]
        q = _heads(jnp.concatenate([ssm_states, hidden_states], axis=-1) @ Wq, H)
        k = _heads(hidden_states @ Wk, HK)
        v = _heads(hidden_states @ Wv, HK)
        ssm_k = _heads(ssm_states @ Wsk, HK)
        ssm_v = _heads(ssm_states @ Wsv, HK)
        rep = lambda x: jnp.repeat(x, G, axis=1)
        kcat = jnp.concatenate([rep(ssm_k), rep(k)], axis=2)
        vcat = jnp.concatenate([rep(ssm_v), rep(v)], axis=2)
        o = _attend(q, kcat, vcat)
        o = o.transpose(0, 2, 1, 3).reshape(B, T, HID)
        return o @ Wo

    def _L0_ffn_ref(x, w_router, w_gate, w_up, w_down, amplitudes, expert_scale, shared_w_gate, shared_w_up, shared_w_down):
        import jax, jax.numpy as jnp
        import numpy as np
        H = 512
        I = 256
        K = 8
        E = 128
        TOPK = 4
        EPS = 1e-08
        B, S, _ = x.shape
        T = B * S
        xt = x.reshape(T, H)
        probs = jax.nn.softmax(xt @ w_router, axis=-1)
        topk_p, topk_idx = jax.lax.top_k(probs, TOPK)
        topk_w = topk_p / (jnp.sum(topk_p, axis=-1, keepdims=True) + EPS)
        gate = (xt @ w_gate).reshape(T, K, I)
        up = (xt @ w_up).reshape(T, K, I)
        basis = jax.nn.silu(gate) * up
        p = amplitudes[..., 0] ** 2 + amplitudes[..., 1] ** 2
        mix = p / (jnp.sum(p, axis=-1, keepdims=True) + EPS)
        mix_sel = mix[topk_idx]
        mixed = jnp.einsum('tek,tki->tei', mix_sel, basis)
        down = jnp.einsum('tei,ih->teh', mixed, w_down)
        coeff = topk_w * expert_scale[topk_idx]
        out = jnp.einsum('teh,te->th', down, coeff)
        shared = jax.nn.silu(xt @ shared_w_gate) * (xt @ shared_w_up) @ shared_w_down
        out = out + shared
        return out.reshape(B, S, H)
    x = x + jnp.tanh(g_xattn[0]) * _L0_xattn_ref(_layernorm(x, axis=-1), ctx_2048, L0_xattn_Wq, L0_xattn_Wk, L0_xattn_Wv, L0_xattn_Wsk, L0_xattn_Wsv, L0_xattn_Wo)
    x = x + jnp.tanh(g_ffn[0]) * _L0_ffn_ref(_layernorm(x, axis=-1), L0_ffn_w_router, L0_ffn_w_gate, L0_ffn_w_up, L0_ffn_w_down, L0_ffn_amplitudes, L0_ffn_expert_scale, L0_ffn_shared_w_gate, L0_ffn_shared_w_up, L0_ffn_shared_w_down)
    return x

_drawn_inputs = setup_inputs


def setup_inputs(seed=0):
    import zlib

    import numpy as np

    out = dict(_drawn_inputs(seed))
    spreads = {'L0_ffn_expert_scale': (1.0, 0.6)}
    factors = {'L0_ffn_w_router': 8.0,
     'L0_ffn_w_gate': 4.714,
     'L0_ffn_w_up': 4.611,
     'L0_ffn_w_down': 4.605,
     'L0_ffn_amplitudes': 8.0,
     'L0_ffn_shared_w_gate': 2.822,
     'L0_ffn_shared_w_up': 2.763,
     'L0_ffn_shared_w_down': 2.768}
    for name, (base, spread) in spreads.items():
        noise = np.random.default_rng([zlib.crc32(name.encode()), seed]).standard_normal(out[name].shape)
        drawn = base * np.exp(spread * noise) if base else spread * noise
        out[name] = jnp.asarray(drawn.astype(out[name].dtype))
    for name, factor in factors.items():
        out[name] = (out[name] * factor).astype(out[name].dtype)
    return out
```

```python
from contextlib import ExitStack

import numpy as np

import concourse.bass as bass
from concourse import mybir

ALU = mybir.AluOpType
ACT = mybir.ActivationFunctionType
AX = mybir.AxisListType
F32 = mybir.dt.float32
F32R = mybir.dt.float32r

P = 128
B, T, HID = 8, 256, 512
H, HK = 32, 8
G = H // HK
D = HID // H
W = 64
NB = T // W
HC = HID // P
TB = T // P
NT = B * TB
UNITS = HK * NB
RING = 4
LN_EPS = 1e-5
MASKED = -3.0e38
PASSES = (("hi", "hi"), ("lo", "hi"), ("hi", "lo"))

E, TOPK, KB, FI = 128, 4, 8, 256
FS = 512
FFN_EPS = 1e-8
NG = 4
GT = B * T // NG


def wait_alone(eng, sem, value, passed):
    eng.wait_ge(sem, value)
    eng.sem_inc(passed, 1)


def newton_rsqrt(dve, done, count, var_eps, root, rstd, tmp):
    def link(ins):
        count[0] += 1
        ins.then_inc(done, 1)
        dve.wait_ge(done, count[0])
    link(dve.reciprocal(rstd, root))
    link(dve.tensor_tensor(tmp, rstd, rstd, ALU.mult))
    link(dve.tensor_tensor(tmp, tmp, var_eps, ALU.mult))
    link(dve.tensor_scalar(tmp, tmp, -0.5, 1.5, ALU.mult, ALU.add))
    link(dve.tensor_tensor(rstd, rstd, tmp, ALU.mult))


def build_attention(nc, ctx, a, X, ident, x1_stats):
    def sb(name, shape, dt=F32):
        return ctx.enter_context(nc.sbuf_tensor(name, shape, dt))

    def ps(name, shape):
        return ctx.enter_context(nc.psum_tensor(name, shape, F32))

    def sem(name):
        return ctx.enter_context(nc.semaphore(name))

    WQ = {h: sb(f"wq_{h}", [P, 2 * HC, HID], F32R) for h in ("hi", "lo")}
    WKV = {h: sb(f"wkv_{h}", [P, 4, HC, P], F32R) for h in ("hi", "lo")}
    WO = {h: sb(f"wo_{h}", [P, HC, HID], F32R) for h in ("hi", "lo")}
    ctx_rows = sb("ctx_rows", [P, TB, HID])
    xn = sb("xn", [P, TB, HID])
    AT = {h: sb(f"actT_{h}", [P, 2 * HC, T], F32R) for h in ("hi", "lo")}
    Q = {h: sb(f"qT_{h}", [P, 2, NB, 2, W], F32R) for h in ("hi", "lo")}
    K = {h: sb(f"kT_{h}", [P, NB, 2, W], F32R) for h in ("hi", "lo")}
    KM = {h: sb(f"kmask_{h}", [P, 2, NB * 2 * W], F32R) for h in ("hi", "lo")}
    VT = sb("vT", [P, NB, 2, W])
    VA = sb("v_ones", [P, NB, HK, 2 * D])
    bias = sb("bias", [P, HK * 2, 4 * W])
    SC = sb("scores_sb", [P, RING, 2, 4 * W])
    NM = sb("neg_max", [P, RING, 2])
    PT = sb("probsT", [P, 2, 2 * NB, G, W])
    OS = sb("oT_sums", [P, T])
    RI = sb("inv_sums", [P, TB, G])
    O = sb("o_rows", [P, TB, HID])
    OT = {h: sb(f"oT_{h}", [P, TB, HC, P], F32R) for h in ("hi", "lo")}
    stage = PT[:, :, :, :, :].rearrange("p b h r q -> p (b h r q)").rearrange("p (s n) -> p s n", s=4)
    rel_pen = SC[:, 0, :, :]
    head_rows = sb("head_rows", [P, HK])
    slopes = sb("slopes", [P, 2 * HK])
    stats = sb("stats", [P, NT, 6])
    mv = sb("mean_var", [P, NT, 2])
    var_eps = sb("var_eps", [P, NT])
    root = sb("root", [P, NT])
    rstd = sb("rstd", [P, NT])
    tmp = sb("tmp", [P, NT])
    eps = sb("eps", [P, 1])
    gate = sb("gate", [P, 1])
    tg = sb("tanh_gate", [P, 1])

    PJ = ps("ps_proj", [P, 2, HID])
    PS = ps("ps_scores", [P, 2, 2, 4 * W])
    PX = ps("ps_probsT", [P, 2, 2, 2, P])
    PO = ps("ps_oT", [P, HID])
    PN = ps("ps_o", [P, HID])

    consts_in, weights_in, x_in, ctx_in = sem("consts_in"), sem("weights_in"), sem("x_in"), sem("ctx_in")
    stage_in = [sem(f"stage_in{s}") for s in range(4)]
    weights_hi, weights_lo, chain, root_done, tg_done = (
        sem("weights_hi"), sem("weights_lo"), sem("chain"), sem("root_done"), sem("tg_done"))
    pool_ready, dve_passed = sem("pool_ready"), sem("dve_passed")
    xn_ready, prep_t, prep_hi, prep_lo = sem("xn_ready"), sem("prep_t"), sem("prep_hi"), sem("prep_lo")
    proj_mm, proj_hi, proj_lo = sem("proj_mm"), sem("proj_hi"), sem("proj_lo")
    v_turned, v_ready, km_ready = sem("v_turned"), sem("v_ready"), sem("km_ready")
    scores_mm, sc_done, exp_done, probs_t = sem("scores_mm"), sem("sc_done"), sem("exp_done"), sem("probs_t")
    pt_done = [sem("pt_done_act"), sem("pt_done_dve")]
    pv_mm, oT_out, o_turned, inv_done, o_done = (
        sem("pv_mm"), sem("oT_out"), sem("o_turned"), sem("inv_done"), sem("o_done"))
    oT_mm, oT_hi, oT_lo, wo_mm, x1_done, st_done = (
        sem("oT_mm"), sem("oT_hi"), sem("oT_lo"), sem("wo_mm"), sem("x1_done"), sem("st_done"))

    x_t = a["x"].rearrange("b (t p) d -> p b t d", p=P)
    ctx_t = a["ctx_2048"].rearrange("b (t p) d -> p b t d", p=P)

    wq_d = a["L0_xattn_Wq"].rearrange("(c p) n -> p c n", p=P)
    wo_d = a["L0_xattn_Wo"].rearrange("(c p) n -> p c n", p=P)
    kv_d = [a[f"L0_xattn_{n}"].rearrange("(c p) n -> p c n", p=P) for n in ("Wsk", "Wk", "Wsv", "Wv")]

    def q_order(part, c):
        return part[:, c, :].rearrange("p (r g d) -> p g r d", r=G, g=HK)

    halves = []
    for c in range(2 * HC):
        halves.append((wq_d[:, c, :], {h: q_order(WQ[h], c) for h in WQ}, ("g r d", dict(g=HK, r=G))))
    for m in range(4):
        halves.append((kv_d[m], {h: WKV[h][:, m] for h in WKV}, ("c n", dict(c=HC))))
    for c in range(HC):
        halves.append((wo_d[:, c, :], {h: WO[h][:, c, :] for h in WO}, None))

    def raw(n):
        v = stage[:, (n // 2) % 4, (n % 2) * HID:(n % 2 + 1) * HID]
        shape = halves[n][2]
        return v.rearrange(f"p ({shape[0]}) -> p {shape[0]}", **shape[1]) if shape else v

    def probs_out(eng, nce, b, u):
        g, i = divmod(u, NB)
        if i < 2 and g >= 2:
            eng.wait_ge(pv_mm, b * HK + g - 1)
        eng.wait_ge(probs_t, b * UNITS + u + 1)
        first = 1 if i == 0 else 0
        dst = PT[:, g % 2, 2 * i + first:2 * i + 2].rearrange("p h r q -> p (h r q)")
        src = PX[:, u % 2, first:2].rearrange("p h k q -> p (h k q)")
        if u % 2 == 0:
            nce.activation(dst, src, ACT.Copy).then_inc(pt_done[0], 1)
        else:
            nce.tensor_copy(dst, src).then_inc(pt_done[1], 1)

    block = ctx.enter_context(nc.Block())

    @block.sync
    def _(sp):
        sp.dma_start(X[:, 0:TB, :], x_t[:, 0]).then_inc(x_in, 16)
        sp.dma_start(ctx_rows[:], ctx_t[:, 0]).then_inc(ctx_in, 16)
        for dst, src in ((ident[:], a["identity"]), (head_rows[:], a["head_rows"]), (slopes[:], a["slopes"]),
                         (rel_pen, a["rel_pen"]), (gate[:], a["g_xattn"].partition_broadcast(P))):
            sp.dma_start(dst, src).then_inc(consts_in, 16)
        for n in range(len(halves)):
            if n >= 8:
                sp.wait_ge(weights_lo, n - 8 + 2 - n % 2)
            src = halves[n][0]
            dst = stage[:, (n // 2) % 4, (n % 2) * HID:(n % 2 + 1) * HID]
            if len(src.shape) == 3:
                dst = dst.rearrange("p (c n) -> p c n", c=HC)
            sp.dma_start(dst, src).then_inc(stage_in[(n // 2) % 4], 16)
            if n < B - 1:
                sp.dma_start(X[:, TB * (n + 1):TB * (n + 2), :], x_t[:, n + 1]).then_inc(x_in, 16)
        with sp.Fori(0, B - 1) as b:
            sp.wait_ge(prep_t, b * 4 + 2)
            sp.dma_start(ctx_rows[:], ctx_t[:, bass.ds(b + 1, 1)].rearrange("p b t d -> p (b t) d")).then_inc(ctx_in, 16)

    @block.gpsimd
    def _(pool):
        pool.memset(VA[:], 1.0).then_inc(pool_ready, 1)
        pool.memset(eps[:], LN_EPS).then_inc(pool_ready, 1)
        pool.wait_ge(consts_in, 80)
        with pool.Fori(0, B) as b:
            for g in range(HK):
                if g == 0:
                    pool.wait_ge(proj_lo, b * 5 + 5)
                if g >= 2:
                    pool.wait_ge(scores_mm, b * UNITS + NB * (g - 1))
                for h in ("hi", "lo"):
                    pool.tensor_tensor(KM[h][:, g % 2, :], K[h][:].bitcast(F32).rearrange("p j s w -> p (j s w)"),
                                       head_rows[:, g:g + 1].broadcast_to([P, NB * 2 * W]),
                                       ALU.mult).then_inc(km_ready, 1)

    @block.scalar
    def _(act):
        act.wait_ge(pool_ready, 2)
        act.wait_ge(consts_in, 80)
        act.activation(tg[:], gate[:], ACT.Tanh).then_inc(tg_done, 1)

        def split_hi(n):
            act.wait_ge(stage_in[(n // 2) % 4], 32 * (n // 8) + 32)
            for_part = halves[n][1]["hi"]
            act.activation(for_part, raw(n), ACT.Copy).then_inc(weights_hi, 1)
        for n in range(8):
            split_hi(n)
        act.wait_ge(st_done, 1)
        act.activation(root[:], var_eps[:], ACT.Sqrt).then_inc(root_done, 1)
        for n in range(8, len(halves)):
            split_hi(n)

        with act.Fori(0, B) as b:
            for i in range(4):
                act.wait_ge(prep_t, b * 4 + i + 1)
                src, t = i // 2, i % 2
                act.activation(AT["hi"][:, src * HC:(src + 1) * HC, t * P:(t + 1) * P],
                               PJ[:, i % 2, :].rearrange("p (c n) -> p c n", c=HC), ACT.Copy).then_inc(prep_hi, 1)
            for n in range(6):
                act.wait_ge(proj_mm, b * 6 + n + 1)
                if n < 4:
                    act.activation(Q["hi"][:, n // 2, :, n % 2, :],
                                   PJ[:, n % 2, 0:T].rearrange("p (i w) -> p i w", i=NB), ACT.Copy).then_inc(proj_hi, 1)
                else:
                    dst = K["hi"] if n == 4 else VT
                    act.activation(dst[:].rearrange("p j s w -> p s j w"),
                                   PJ[:, n % 2, :].rearrange("p (s j w) -> p s j w", s=2, j=NB),
                                   ACT.Copy).then_inc(proj_hi, 1)
            for s in range(UNITS + 12):
                if s < UNITS:
                    i = s % NB
                    n = 2 * W if i == 0 else 4 * W
                    for pp in range(2):
                        act.wait_ge(sc_done, b * 2 * UNITS + 2 * s + pp + 1)
                        act.activation(SC[:, s % RING, pp, 0:n], SC[:, s % RING, pp, 0:n], ACT.Exp,
                                       bias=NM[:, s % RING, pp:pp + 1], scale=-1.0).then_inc(exp_done, 1)
                u = s - 3
                if 0 <= u < UNITS and u % 2 == 0:
                    probs_out(act, nc.scalar, b, u)
                g, r = divmod(s - 8, NB)
                if r == 0 and 0 <= g < HK:
                    act.wait_ge(pv_mm, b * HK + g + 1)
                    if g >= 1:
                        act.wait_ge(o_turned, b * HK + g)
                    act.activation(OS[:], PO[:, 0:T], ACT.Copy).then_inc(oT_out, 1)
            for t in range(TB):
                act.wait_ge(oT_mm, b * TB + t + 1)
                act.activation(OT["hi"][:, t], PJ[:, t, :].rearrange("p (c n) -> p c n", c=HC),
                               ACT.Copy).then_inc(oT_hi, 1)

    @block.vector
    def _(dve):
        count = [0]

        def link(ins):
            count[0] += 1
            ins.then_inc(chain, 1)
            dve.wait_ge(chain, count[0])

        dve.wait_ge(consts_in, 80)
        for k in range(2 * HK):
            ins = dve.scalar_tensor_tensor(out=bias[:, k, :], in0=rel_pen[:, 0, :], scalar=slopes[:, k:k + 1],
                                           in1=rel_pen[:, 1, :], op0=ALU.mult, op1=ALU.add)
        link(ins)

        def split_lo(n):
            dve.wait_ge(weights_hi, n + 1)
            dve.tensor_tensor(halves[n][1]["lo"], raw(n), halves[n][1]["hi"].bitcast(F32),
                              ALU.subtract).then_inc(weights_lo, 1)
        for n in range(8):
            split_lo(n)
        for t in range(NT):
            dve.wait_ge(x_in, 16 * (t // TB + 1))
            link(dve.bn_stats(stats[:, t, :], X[:, t, :]))
            ins = dve.bn_aggr(mv[:, t, :], stats[:, t, :])
        link(ins)
        dve.wait_ge(pool_ready, 2)
        link(dve.tensor_scalar(var_eps[:], mv[:, :, 1], LN_EPS, None, ALU.add))
        dve.tensor_copy(tmp[:], var_eps[:]).then_inc(st_done, 1)
        dve.wait_ge(root_done, 1)
        newton_rsqrt(dve, chain, count, var_eps[:], root[:], rstd[:], tmp[:])
        for n in range(8, len(halves)):
            split_lo(n)
        dve.wait_ge(tg_done, 1)

        with dve.Fori(0, B) as b:
            for t in range(TB):
                dve.tensor_scalar(xn[:, t, :], X[:, bass.ds(b * TB + t, 1), :].rearrange("p o d -> p (o d)"),
                                  mv[:, bass.ds(b * TB + t, 1), 0], rstd[:, bass.ds(b * TB + t, 1)],
                                  ALU.subtract, ALU.mult).then_inc(xn_ready, 1)
            for i in range(4):
                dve.wait_ge(prep_hi, b * 4 + i + 1)
                src, t = i // 2, i % 2
                where = (slice(None), slice(src * HC, (src + 1) * HC), slice(t * P, (t + 1) * P))
                dve.tensor_tensor(AT["lo"][where], PJ[:, i % 2, :].rearrange("p (c n) -> p c n", c=HC),
                                  AT["hi"][where].bitcast(F32), ALU.subtract).then_inc(prep_lo, 1)
            for n in range(5):
                dve.wait_ge(proj_hi, b * 6 + n + 1)
                if n < 4:
                    dve.tensor_tensor(Q["lo"][:, n // 2, :, n % 2, :],
                                      PJ[:, n % 2, 0:T].rearrange("p (i w) -> p i w", i=NB),
                                      Q["hi"][:, n // 2, :, n % 2, :].bitcast(F32), ALU.subtract).then_inc(proj_lo, 1)
                else:
                    dve.tensor_tensor(K["lo"][:].rearrange("p j s w -> p s j w"),
                                      PJ[:, n % 2, :].rearrange("p (s j w) -> p s j w", s=2, j=NB),
                                      K["hi"][:].bitcast(F32).rearrange("p j s w -> p s j w"),
                                      ALU.subtract).then_inc(proj_lo, 1)
            dve.wait_ge(v_turned, b + 1)
            dve.tensor_copy(VA[:, :, :, 0:D], PJ[:, 0, :].rearrange("p (j g d) -> p j g d", j=NB, g=HK)
                            ).then_inc(v_ready, 1)
            for s in range(UNITS + 12):
                if s < UNITS:
                    g, i = divmod(s, NB)
                    n = 2 * W if i == 0 else 4 * W
                    if s >= RING:
                        dve.wait_ge(probs_t, b * UNITS + s - RING + 1)
                    wait_alone(dve, scores_mm, b * UNITS + s + 1, dve_passed)
                    for pp in range(2):
                        dve.tensor_tensor_reduce(SC[:, s % RING, pp, 0:n], PS[:, s % 2, pp, 0:n],
                                                 bias[:, 2 * g + pp, 4 * W - n:4 * W], -float(D) ** -0.5, 3e38,
                                                 ALU.add, ALU.min, NM[:, s % RING, pp:pp + 1]).then_inc(sc_done, 1)
                u = s - 3
                if 0 <= u < UNITS and u % 2 == 1:
                    probs_out(dve, nc.vector, b, u)
                g, r = divmod(s - 10, NB)
                if r == 0 and 0 <= g < HK:
                    dve.wait_ge(o_turned, b * HK + g + 1)
                    v = PN[:, 0:T].rearrange("p (t r e) -> p t r e", t=TB, r=G)
                    dve.reciprocal(RI[:], v[:, :, :, D]).then_inc(inv_done, 1)
                    dve.wait_ge(inv_done, b * HK + g + 1)
                    dve.tensor_tensor(O[:, :, g * G * D:(g + 1) * G * D].rearrange("p t (r d) -> p t r d", r=G),
                                      v[:, :, :, 0:D], RI[:].unsqueeze(3).broadcast_to([P, TB, G, D]),
                                      ALU.mult).then_inc(o_done, 1)
            for t in range(TB):
                dve.wait_ge(oT_hi, b * TB + t + 1)
                dve.tensor_tensor(OT["lo"][:, t], PJ[:, t, :].rearrange("p (c n) -> p c n", c=HC),
                                  OT["hi"][:, t].bitcast(F32), ALU.subtract).then_inc(oT_lo, 1)
            for t in range(TB):
                row = X[:, bass.ds(b * TB + t, 1), :].rearrange("p o d -> p (o d)")
                dve.wait_ge(wo_mm, b * TB + t + 1)
                dve.scalar_tensor_tensor(out=row, in0=PS[:, t].rearrange("p k n -> p (k n)"), scalar=tg[:, 0:1],
                                         in1=row, op0=ALU.mult, op1=ALU.add).then_inc(x1_done, 1)
                dve.wait_ge(x1_done, b * TB + t + 1)
                dve.bn_stats(x1_stats[:, bass.ds(b * TB + t, 1), :].rearrange("p o d -> p (o d)"), row)

    @block.tensor
    def _(pe):
        pe.wait_ge(consts_in, 80)
        pe.wait_ge(weights_lo, len(halves))

        def proj(out, stat, mov, chunks):
            n = [(c, s, m) for c in chunks for s, m in PASSES]
            for j, (c, s, m) in enumerate(n):
                ins = pe.matmul(out, stat(s, c), mov(m, c), start=j == 0, stop=j == len(n) - 1)
            return ins

        def score(b, s):
            g, i = divmod(s, NB)
            n = 2 * W if i == 0 else 4 * W
            if i == 0:
                pe.wait_ge(km_ready, b * 2 * HK + 2 * (g + 1))
            if s >= 2:
                pe.wait_ge(sc_done, b * 2 * UNITS + 2 * (s - 1))
            for pp in range(2):
                for j, (sp_, mp) in enumerate(PASSES):
                    ins = pe.matmul(PS[:, s % 2, pp, 0:n], Q[sp_][:, pp, i].rearrange("p r w -> p (r w)"),
                                    KM[mp][:, g % 2, (i + 1) * 2 * W - n:(i + 1) * 2 * W],
                                    start=j == 0, stop=j == 2)
            ins.then_inc(scores_mm, 1)

        def turn_probs(b, u):
            g, i = divmod(u, NB)
            pe.wait_ge(exp_done, b * 2 * UNITS + 2 * u + 2)
            if u >= 2:
                pe.wait_ge(pt_done[u % 2], b * UNITS // 2 + u // 2)
            first = 1 if i == 0 else 0
            for h in range(first, 2):
                for pp in range(2):
                    ins = pe.transpose(PX[:, u % 2, h, pp, :], SC[:, u % RING, pp, (h - first) * P:(h - first + 1) * P],
                                       ident[:])
            ins.then_inc(probs_t, 1)

        def times_v(b, g):
            if g == 0:
                pe.wait_ge(v_ready, b + 1)
            for e in range(2):
                pe.wait_ge(pt_done[e], b * UNITS // 2 + 2 * (g + 1))
            if g >= 1:
                pe.wait_ge(oT_out, b * HK + g)
            for j in range(NB):
                n = min(2 * W, T - j * W)
                for r in range(G):
                    ins = pe.matmul(PO[32 * r:32 * r + 2 * D, j * W:j * W + n], VA[:, j, g, :],
                                    PT[:, g % 2, 2 * j + 1:2 * j + 1 + n // W, r, :],
                                    start=j == 0, stop=j == NB - 1, skip_group_check=True)
            ins.then_inc(pv_mm, 1)

        def turn_o(b, g):
            pe.wait_ge(oT_out, b * HK + g + 1)
            if g >= 1:
                pe.wait_ge(o_done, b * HK + g)
            for t in range(TB):
                ins = pe.transpose(PN[:, t * P:(t + 1) * P], OS[:, t * P:(t + 1) * P], ident[:])
            ins.then_inc(o_turned, 1)

        with pe.Fori(0, B) as b:
            for i in range(4):
                src, t = i // 2, i % 2
                if src == 0:
                    pe.wait_ge(ctx_in, b * 16 + 16)
                else:
                    pe.wait_ge(xn_ready, b * TB + t + 1)
                if i >= 2:
                    pe.wait_ge(prep_lo, b * 4 + i - 1)
                rows = ctx_rows if src == 0 else xn
                for c in range(HC):
                    ins = pe.transpose(PJ[:, i % 2, c * P:(c + 1) * P], rows[:, t, c * P:(c + 1) * P], ident[:])
                ins.then_inc(prep_t, 1)
            pe.wait_ge(prep_lo, b * 4 + 4)
            for n in range(4):
                if n >= 2:
                    pe.wait_ge(proj_lo, b * 5 + n - 1)
                proj(PJ[:, n % 2, 0:T], lambda h, c: WQ[h][:, c, n * P:(n + 1) * P], lambda h, c: AT[h][:, c, :],
                     range(2 * HC)).then_inc(proj_mm, 1)
            for n in range(4, 6):
                pe.wait_ge(proj_lo, b * 5 + n - 1)
                for src in range(2):
                    ins = proj(PJ[:, n % 2, src * T:(src + 1) * T],
                               lambda h, c: WKV[h][:, 2 * (n - 4) + src, c, :],
                               lambda h, c: AT[h][:, src * HC + c, :], range(HC))
                ins.then_inc(proj_mm, 1)
            pe.wait_ge(proj_hi, b * 6 + 6)
            pe.wait_ge(proj_lo, b * 5 + 5)
            for j in range(NB):
                ins = pe.transpose(PJ[:, 0, j * P:(j + 1) * P], VT[:, j].rearrange("p s w -> p (s w)"), ident[:])
            ins.then_inc(v_turned, 1)
            for s in range(UNITS + 12):
                if s < UNITS:
                    score(b, s)
                if 0 <= s - 2 < UNITS:
                    turn_probs(b, s - 2)
                g, r = divmod(s - 7, NB)
                if r == 0 and 0 <= g < HK:
                    times_v(b, g)
                g, r = divmod(s - 9, NB)
                if r == 0 and 0 <= g < HK:
                    turn_o(b, g)
            pe.wait_ge(o_done, b * HK + HK)
            for t in range(TB):
                for c in range(HC):
                    ins = pe.transpose(PJ[:, t, c * P:(c + 1) * P], O[:, t, c * P:(c + 1) * P], ident[:])
                ins.then_inc(oT_mm, 1)
            for t in range(TB):
                pe.wait_ge(oT_lo, b * TB + t + 1)
                proj(PS[:, t].rearrange("p k n -> p (k n)"), lambda h, c: OT[h][:, t, c, :],
                     lambda h, c: WO[h][:, c, :], range(HC)).then_inc(wo_mm, 1)


def build_ffn(nc, ctx, a, X, ident, x1_stats, out):
    def sb(name, shape, dt=F32):
        return ctx.enter_context(nc.sbuf_tensor(name, shape, dt))

    def ps(name, shape):
        return ctx.enter_context(nc.psum_tensor(name, shape, F32))

    def sem(name):
        return ctx.enter_context(nc.semaphore(name))

    TOK = B * T
    XT = {h: sb(f"xnT_{h}", [P, HC, TOK], F32R) for h in ("hi", "lo")}
    big = sb("big", [P, 4, TOK])
    hT = big[:, :, :]
    mixed, cB = big[:, 0:2, :], big[:, 2, :]
    WB = {h: sb(f"w_{h}", [P, 2, 2, 4 * P], F32R) for h in ("hi", "lo")}
    raw = sb("w_raw", [P, 2, 2, 4 * P])
    DL = {h: sb(f"down_{h}", [P, 2, 4, P], F32R) for h in ("hi", "lo")}
    PR_ = sb("probs", [P, NT, E + 4])
    left = sb("probs_left", [P, NT * (E + 4)])
    probs_left = left[:, :].rearrange("p (t e) -> p t e", t=NT)
    coeffT = left[:, 0:TOK]
    SG = sb("silu_gate", [P, 2, GT])
    BS = sb("basis", [P, 2, GT])
    xn, logitsT = BS, SG
    MR = sb("mix_column", [P, P])
    amp = sb("amp", [P, KB, 2])
    amp2 = sb("amp2", [P, KB])
    mix = sb("mix", [P, KB])
    escale = sb("escale", [P, 1])
    col = {n: sb(n, [P, 1]) for n in ("mix_sum", "gate_f", "tanh_gate_f")}
    mv = sb("mean_var1", [P, NT, 2])
    ln = {n: sb(n, [P, NT]) for n in ("var_eps1", "root1", "rstd1", "tmp1")}
    top8 = sb("top8", [P, NT, 8])
    per_tile = {n: sb(n, [P, NT]) for n in ("row_max", "row_sum", "row_inv", "top_sum", "top_inv")}

    PT = ps("ps_turn", [P, 2, GT])
    PG = ps("ps_gate", [P, 2, GT])
    PU = ps("ps_up", [P, 2, GT])

    consts_in, chain, root_done, tg_done = sem("f_consts"), sem("f_chain"), sem("f_root"), sem("f_tg")
    ve_done, ready = sem("f_var"), sem("f_ready")
    raw_in = [sem("raw_in0"), sem("raw_in1")]
    w_hi, w_lo = sem("w_hi_done"), sem("w_lo_done")
    xn_ready, xn_t, xT_hi, xT_lo = sem("f_xn"), sem("f_xnT"), sem("f_xT_hi"), sem("f_xT_lo")
    router_mm, logits_out, logits_t, logits_in = sem("router_mm"), sem("logits_out"), sem("logits_t"), sem("logits_in")
    shifted, exp_done, coeff_done, coeff_t, coeff_out = (
        sem("shifted"), sem("f_exp"), sem("coeff_done"), sem("coeff_t"), sem("coeff_out"))
    gate_mm, up_mm, silu_done, prod_done, basis_done, acc_done = (
        sem("gate_mm"), sem("up_mm"), sem("silu_done"), sem("prod_done"), sem("basis_done"), sem("acc_done"))
    mr_ready, cb_mm, cb_out = sem("mr_ready"), sem("cb_mm"), sem("cb_out")
    sd_hi, sd_lo, sd_mm, sd_out = sem("sd_hi"), sem("sd_lo"), sem("sd_mm"), sem("sd_out")
    d_hi, d_lo, d_mm, d_out, stored = sem("d_hi"), sem("d_lo"), sem("d_mm"), sem("d_out"), sem("stored")

    NS, NE = FS // P, KB * FI // P
    SHARED, SDOWN, EXPERT = 1, 1 + NS, 3 + NS
    DOWN = EXPERT + NE
    HALF = FI // P

    def cols(w, n):
        return w.rearrange("(c p) n -> p c n", p=P)[:, :, bass.ds(n * P, P)]

    block = ctx.enter_context(nc.Block())

    @block.sync
    def _(sp):
        for dst, src in ((amp[:], a["L0_ffn_amplitudes"]), (escale[:], a["L0_ffn_expert_scale"].rearrange("(e o) -> e o", o=1)),
                         (col["gate_f"][:], a["g_ffn"].partition_broadcast(P))):
            sp.dma_start(dst, src).then_inc(consts_in, 16)

        def load(idx, slot, first, second):
            if not isinstance(idx, int) or idx >= 2:
                sp.wait_ge(w_lo, (idx - 1) * 2)
            sp.dma_start(raw[:, slot, 0, :].rearrange("p (c n) -> p c n", c=first.shape[1])
                         if first.shape[1] * first.shape[2] == 4 * P else
                         raw[:, slot, 0, 0:2 * P].rearrange("p (c n) -> p c n", c=2), first).then_inc(raw_in[slot], 16)
            sp.dma_start(raw[:, slot, 1, :].rearrange("p (c n) -> p c n", c=second.shape[1])
                         if second.shape[1] * second.shape[2] == 4 * P else
                         raw[:, slot, 0, 2 * P:4 * P].rearrange("p (c n) -> p c n", c=2), second).then_inc(raw_in[slot], 16)

        router = cols(a["L0_ffn_w_router"], 0)
        load(0, 0, router[:, 0:2], router[:, 2:4])
        for n in range(NS):
            load(SHARED + n, (SHARED + n) % 2, cols(a["L0_ffn_shared_w_gate"], n), cols(a["L0_ffn_shared_w_up"], n))
        sdown = a["L0_ffn_shared_w_down"].rearrange("(c p) n -> p c n", p=P)
        for n in range(2):
            load(SDOWN + n, (SDOWN + n) % 2, sdown[:, 2 * n:2 * n + 1], sdown[:, 2 * n + 1:2 * n + 2])
        with sp.Fori(0, KB) as k:
            for i in range(HALF):
                load(k * HALF + EXPERT + i, (EXPERT + i) % 2, cols(a["L0_ffn_w_gate"], k * HALF + i),
                     cols(a["L0_ffn_w_up"], k * HALF + i))
        down = a["L0_ffn_w_down"].rearrange("(c p) n -> p c n", p=P)
        load(DOWN, DOWN % 2, down[:, 0:1], down[:, 1:2])
        out_t = out.rearrange("b (t p) d -> p (b t) d", p=P)
        with sp.Fori(0, NT) as t:
            sp.wait_ge(d_out, t + 1)
            sp.dma_start(out_t[:, bass.ds(t, 1)], X[:, bass.ds(t, 1), :]).then_inc(stored, 16)
        sp.wait_ge(stored, 16 * NT)

    def at_tile(view, t):
        return view[:, :, bass.ds(t * P, P)]

    @block.gpsimd
    def _(pool):
        pool.memset(PR_[:, :, E:E + 4], -5.0).then_inc(ready, 1)

        def split_lo(idx, slot, width=4 * P):
            pool.wait_ge(w_hi, idx * 2 + 2)
            for half in range(2):
                h, lo = (half, 0) if width == 4 * P else (0, half * width)
                where = (slice(None), slot, h, slice(lo, lo + width))
                pool.tensor_tensor(WB["lo"][where], raw[where], WB["hi"][where].bitcast(F32),
                                   ALU.subtract).then_inc(w_lo, 1)
        split_lo(0, 0, 2 * P)
        for idx in range(1, EXPERT + 1):
            split_lo(idx, idx % 2)
        pool.wait_ge(sd_hi, NT)
        pool.wait_ge(sd_lo, NT)
        pool.memset(mixed, 0.0).then_inc(ready, 1)
        pool.wait_ge(ready, 2)

        def add_up(e, i):
            for t in range(NG):
                pool.wait_ge(basis_done, e * NG + t + 1)
                dst = mixed[:, i, t * GT:(t + 1) * GT]
                pool.tensor_tensor(dst, dst, BS[:, t % 2, :], ALU.add).then_inc(acc_done, 1)

        with pool.Fori(0, KB) as k:
            for i in range(HALF):
                split_lo(k * HALF + EXPERT + 1 + i, (EXPERT + 1 + i) % 2)
                add_up(k * HALF + i, i)

    @block.scalar
    def _(act):
        def split_hi(idx, slot, used=None, width=4 * P):
            act.wait_ge(raw_in[slot], (idx - slot) * 16 + 32)
            if used:
                act.wait_ge(*used)
            for half in range(2):
                h, lo = (half, 0) if width == 4 * P else (0, half * width)
                where = (slice(None), slot, h, slice(lo, lo + width))
                act.activation(WB["hi"][where], raw[where], ACT.Copy).then_inc(w_hi, 1)

        act.wait_ge(consts_in, 48)
        act.activation(col["tanh_gate_f"][:], col["gate_f"][:], ACT.Tanh).then_inc(tg_done, 1)
        split_hi(0, 0, width=2 * P)
        split_hi(1, 1)
        act.wait_ge(ve_done, 1)
        act.activation(ln["root1"][:], ln["var_eps1"][:], ACT.Sqrt).then_inc(root_done, 1)
        with act.Fori(0, NT // 2) as p:
            for s in range(2):
                act.wait_ge(xn_t, p * 2 + s + 1)
                act.activation(at_tile(XT["hi"], p * 2 + s), PT[:, s, :].rearrange("p (c n) -> p c n", c=HC),
                               ACT.Copy).then_inc(xT_hi, 1)
        for q in range(NG):
            act.wait_ge(router_mm, q + 1)
            if q >= 2:
                act.wait_ge(logits_t, q - 1)
            act.activation(logitsT[:, q % 2, :], PG[:, q % 2, :], ACT.Copy).then_inc(logits_out, 1)

        def silu(n, t):
            q = n * NG + t
            act.wait_ge(gate_mm, q + 1)
            if not isinstance(q, int) or q >= 2:
                act.wait_ge(prod_done, q - 1)
            act.activation(SG[:, t % 2, :], PG[:, t % 2, :], ACT.Silu).then_inc(silu_done, 1)

        for n in range(NS):
            for t in range(NG):
                if n == 0 and t == 0:
                    act.wait_ge(logits_t, NG)
                silu(n, t)
                if t == 1:
                    split_hi(SHARED + n + 1, (SHARED + n + 1) % 2,
                             (router_mm, NG) if n == 0 else (up_mm, n * NG))
                if n == 0 and t == NG - 1:
                    act.wait_ge(shifted, 1)
                    act.activation(PR_[:, :, 0:E], PR_[:, :, 0:E], ACT.Exp).then_inc(exp_done, 1)
        split_hi(SDOWN + 1, (SDOWN + 1) % 2, (up_mm, NS * NG))

        def split_rows(src, chunks, done, mm, t, s):
            if not isinstance(t, int) or t >= 2:
                act.wait_ge(mm, t - 1)
            act.activation(DL["hi"][:, s, 0:chunks, :], at_tile(src, t), ACT.Copy).then_inc(done, 1)

        act.wait_ge(prod_done, NS * NG)
        for s in range(2):
            split_rows(hT, 4, sd_hi, sd_mm, s, s)
        with act.Fori(1, NT // 2) as p:
            for s in range(2):
                split_rows(hT, 4, sd_hi, sd_mm, p * 2 + s, s)
        split_hi(EXPERT, EXPERT % 2, (sd_mm, NT))
        for q in range(NG):
            act.wait_ge(coeff_t, q + 1)
            act.activation(coeffT[:, q * GT:(q + 1) * GT], PT[:, q % 2, :], ACT.Copy).then_inc(coeff_out, 1)

        def c_out(k, t):
            act.wait_ge(cb_mm, k * NG + t + 1)
            if not isinstance(k, int) or k >= 1:
                act.wait_ge(basis_done, (k - 1) * HALF * NG + (HALF - 1) * NG + t + 1)
            act.activation(cB[:, t * GT:(t + 1) * GT], PT[:, t % 2, :], ACT.Copy).then_inc(cb_out, 1)

        act.wait_ge(sd_hi, NT)
        act.wait_ge(sd_lo, NT)
        for t in range(NG):
            c_out(0, t)

        def experts(k, last):
            for i in range(HALF):
                for t in range(NG):
                    silu(k * HALF + NS + i, t)
                    if t == 1:
                        split_hi(k * HALF + EXPERT + i + 1, (EXPERT + i + 1) % 2,
                                 (up_mm, (k * HALF + NS + i) * NG))
                    if i == HALF - 1 and not last:
                        c_out(k + 1, t)
        with act.Fori(0, KB - 1) as k:
            experts(k, False)
        experts(KB - 1, True)
        act.wait_ge(acc_done, NE * NG)
        for s in range(2):
            split_rows(mixed, 2, d_hi, d_mm, s, s)
        with act.Fori(1, NT // 2) as p:
            for s in range(2):
                split_rows(mixed, 2, d_hi, d_mm, p * 2 + s, s)

    @block.vector
    def _(dve):
        count = [0]

        def link(ins):
            count[0] += 1
            ins.then_inc(chain, 1)
            dve.wait_ge(chain, count[0])

        for t in range(NT):
            ins = dve.bn_aggr(mv[:, t, :], x1_stats[:, t, :])
        link(ins)
        link(dve.tensor_scalar(ln["var_eps1"][:], mv[:, :, 1], LN_EPS, None, ALU.add))
        dve.tensor_copy(ln["tmp1"][:], ln["var_eps1"][:]).then_inc(ve_done, 1)
        dve.wait_ge(consts_in, 48)
        link(dve.tensor_tensor(amp[:], amp[:], amp[:], ALU.mult))
        link(dve.tensor_tensor(amp2[:], amp[:, :, 0], amp[:, :, 1], ALU.add))
        link(dve.tensor_reduce(col["mix_sum"][:], amp2[:], AX.X, ALU.add))
        link(dve.tensor_scalar(col["mix_sum"][:], col["mix_sum"][:], FFN_EPS, None, ALU.add))
        link(dve.reciprocal(col["mix_sum"][:], col["mix_sum"][:]))
        link(dve.tensor_scalar(mix[:], amp2[:], col["mix_sum"][:, 0:1], escale[:, 0:1], ALU.mult, ALU.mult))
        dve.wait_ge(root_done, 1)
        newton_rsqrt(dve, chain, count, ln["var_eps1"][:], ln["root1"][:], ln["rstd1"][:], ln["tmp1"][:])
        with dve.Fori(0, NT // 2) as p:
            for s in range(2):
                one = bass.ds(p * 2 + s, 1)
                dve.tensor_scalar(xn[:, s, :], X[:, one, :].rearrange("p o d -> p (o d)"), mv[:, one, 0],
                                  ln["rstd1"][:, one], ALU.subtract, ALU.mult).then_inc(xn_ready, 1)
            for s in range(2):
                dve.wait_ge(xT_hi, p * 2 + s + 1)
                dve.tensor_tensor(at_tile(XT["lo"], p * 2 + s), PT[:, s, :].rearrange("p (c n) -> p c n", c=HC),
                                  at_tile(XT["hi"], p * 2 + s).bitcast(F32), ALU.subtract).then_inc(xT_lo, 1)
        dve.wait_ge(ready, 1)
        for q in range(NG):
            dve.wait_ge(logits_t, q + 1)
            dve.tensor_copy(PR_[:, q * 4:(q + 1) * 4, 0:E], PT[:, q % 2, :].rearrange("p (t e) -> p t e", e=E)
                            ).then_inc(logits_in, 1)

        def times(n, t, dst):
            q = n * NG + t
            dve.wait_ge(silu_done, q + 1)
            dve.wait_ge(up_mm, q + 1)
            return dve.tensor_tensor(dst, PU[:, t % 2, :], SG[:, t % 2, :], ALU.mult).then_inc(prod_done, 1)

        probs = PR_[:, :, 0:E]

        def over(v):
            return v.unsqueeze(2).broadcast_to([P, NT, E])

        def top_experts(step):
            w = per_tile
            if step == 0:
                dve.wait_ge(logits_in, NG)
                link(dve.tensor_reduce(w["row_max"][:], probs, AX.X, ALU.max))
            elif step == 1:
                dve.tensor_tensor(probs, probs, over(w["row_max"][:]), ALU.subtract).then_inc(shifted, 1)
            elif step == 4:
                dve.wait_ge(exp_done, 1)
                link(dve.tensor_reduce(w["row_sum"][:], probs, AX.X, ALU.add))
                link(dve.reciprocal(w["row_inv"][:], w["row_sum"][:]))
            elif step == 5:
                link(dve.tensor_tensor(probs, probs, over(w["row_inv"][:]), ALU.mult))
            elif step in (6, 7):
                for t in range((step - 6) * 8, (step - 5) * 8):
                    ins = dve.max(top8[:, t, :], PR_[:, t, 0:E])
                link(ins)
            elif step == 8:
                link(dve.tensor_reduce(w["top_sum"][:], top8[:, :, 0:TOPK], AX.X, ALU.add))
                link(dve.tensor_scalar(w["top_sum"][:], w["top_sum"][:], FFN_EPS, None, ALU.add))
                link(dve.reciprocal(w["top_inv"][:], w["top_sum"][:]))
                link(dve.memset(top8[:, :, TOPK:8], -5.0))
            elif step in (9, 10):
                for t in range((step - 9) * 8, (step - 8) * 8):
                    ins = dve.match_replace(probs_left[:, t, :], top8[:, t, :], PR_[:, t, :], 0.0)
                link(ins)
            elif step == 11:
                link(dve.tensor_tensor(probs, probs, probs_left[:, :, 0:E], ALU.subtract))
            elif step == 12:
                dve.tensor_tensor(probs, probs, over(w["top_inv"][:]), ALU.mult).then_inc(coeff_done, 1)

        for n in range(NS):
            for t in range(NG):
                times(n, t, hT[:, n, t * GT:(t + 1) * GT])
                top_experts(n * NG + t)
        dve.wait_ge(tg_done, 1)

        def rest_rows(src, chunks, hi, lo, t, s):
            dve.wait_ge(hi, t + 1)
            dve.tensor_tensor(DL["lo"][:, s, 0:chunks, :], at_tile(src, t), DL["hi"][:, s, 0:chunks, :].bitcast(F32),
                              ALU.subtract).then_inc(lo, 1)

        def add_rows(mm, done, t, s):
            row = X[:, bass.ds(t, 1), :].rearrange("p o d -> p (o d)")
            dve.wait_ge(mm, t + 1)
            dve.scalar_tensor_tensor(out=row, in0=PT[:, s, :], scalar=col["tanh_gate_f"][:, 0:1], in1=row,
                                     op0=ALU.mult, op1=ALU.add).then_inc(done, 1)

        def down(src, chunks, hi, lo, mm, done):
            for s in range(2):
                rest_rows(src, chunks, hi, lo, s, s)
            with dve.Fori(1, NT // 2) as p:
                for s in range(2):
                    add_rows(mm, done, p * 2 + s - 2, s)
                    rest_rows(src, chunks, hi, lo, p * 2 + s, s)
            for s in range(2):
                add_rows(mm, done, NT - 2 + s, s)

        down(hT, 4, sd_hi, sd_lo, sd_mm, sd_out)

        def mix_column(k):
            if not isinstance(k, int) or k >= 1:
                dve.wait_ge(cb_mm, k * NG)
            dve.tensor_copy(MR[:], mix[:, bass.ds(k, 1)].broadcast_to([P, P])).then_inc(mr_ready, 1)

        mix_column(0)

        def experts(k, last):
            for i in range(HALF):
                for t in range(NG):
                    e = k * HALF + i
                    q = e * NG + t
                    if not isinstance(q, int) or q >= 2:
                        dve.wait_ge(acc_done, q - 1)
                    times(e + NS, t, BS[:, t % 2, :])
                    if i == 0:
                        dve.wait_ge(cb_out, k * NG + t + 1)
                    dve.wait_ge(prod_done, (e + NS) * NG + t + 1)
                    dve.tensor_tensor(BS[:, t % 2, :], BS[:, t % 2, :], cB[:, t * GT:(t + 1) * GT],
                                      ALU.mult).then_inc(basis_done, 1)
                if i == 0 and not last:
                    mix_column(k + 1)
        experts(0, False)
        with dve.Fori(1, KB - 1) as k:
            experts(k, False)
        experts(KB - 1, True)
        down(mixed, 2, d_hi, d_lo, d_mm, d_out)

    @block.tensor
    def _(pe):
        with pe.Fori(0, NT // 2) as p:
            for s in range(2):
                pe.wait_ge(xn_ready, p * 2 + s + 1)
                for c in range(HC):
                    ins = pe.transpose(PT[:, s, c * P:(c + 1) * P], xn[:, s, c * P:(c + 1) * P], ident[:])
                ins.then_inc(xn_t, 1)

        def proj(out, stat, mov, chunks):
            n = [(c, s, m) for c in range(chunks) for s, m in PASSES]
            for j, (c, s, m) in enumerate(n):
                ins = pe.matmul(out, stat(s, c), mov(m, c), start=j == 0, stop=j == len(n) - 1)
            return ins

        def tokens(t):
            return lambda h, c: XT[h][:, c, t * GT:(t + 1) * GT]

        def weights(slot, half):
            return lambda h, c: WB[h][:, slot, half, c * P:(c + 1) * P]

        pe.wait_ge(xT_lo, NT)
        pe.wait_ge(w_lo, 2)

        def turn_logits(q):
            pe.wait_ge(logits_out, q + 1)
            if q >= 2:
                pe.wait_ge(logits_in, q - 1)
            for j in range(4):
                ins = pe.transpose(PT[:, q % 2, j * P:(j + 1) * P], logitsT[:, q % 2, j * P:(j + 1) * P], ident[:])
            ins.then_inc(logits_t, 1)

        for q in range(NG):
            if q >= 2:
                pe.wait_ge(logits_out, q - 1)
            ins = proj(PG[:, q % 2, :], weights(0, 0), tokens(q), HC).then_inc(router_mm, 1)
            if q >= 1:
                turn_logits(q - 1)
        turn_logits(NG - 1)

        def gate_up(n, slot, t):
            q = n * NG + t
            if not isinstance(q, int) or q >= 2:
                pe.wait_ge(silu_done, q - 1)
            proj(PG[:, t % 2, :], weights(slot, 0), tokens(t), HC).then_inc(gate_mm, 1)
            if not isinstance(q, int) or q >= 2:
                pe.wait_ge(prod_done, q - 1)
            proj(PU[:, t % 2, :], weights(slot, 1), tokens(t), HC).then_inc(up_mm, 1)

        for n in range(NS):
            pe.wait_ge(w_lo, 2 * (SHARED + n) + 2)
            for t in range(NG):
                gate_up(n, (SHARED + n) % 2, t)

        def down(chunks, weight, lo, mm, done, t, s):
            pe.wait_ge(lo, t + 1)
            if not isinstance(t, int) or t >= 2:
                pe.wait_ge(done, t - 1)
            return proj(PT[:, s, :], lambda h, c: DL[h][:, s, c, :], weight, chunks).then_inc(mm, 1)

        def sdown_w(h, c):
            return WB[h][:, (SDOWN + c // 2) % 2, c % 2, :]

        pe.wait_ge(w_lo, 2 * SDOWN + 4)
        for s in range(2):
            down(4, sdown_w, sd_lo, sd_mm, sd_out, s, s)
        with pe.Fori(1, NT // 2 - 1) as p:
            for s in range(2):
                down(4, sdown_w, sd_lo, sd_mm, sd_out, p * 2 + s, s)
        down(4, sdown_w, sd_lo, sd_mm, sd_out, NT - 2, 0)
        down(4, sdown_w, sd_lo, sd_mm, sd_out, NT - 1, 1)
        pe.wait_ge(coeff_done, 1)
        pe.wait_ge(sd_out, NT)
        for q in range(NG):
            if q >= 2:
                pe.wait_ge(coeff_out, q - 1)
            for j in range(4):
                ins = pe.transpose(PT[:, q % 2, j * P:(j + 1) * P], PR_[:, q * 4 + j, 0:E], ident[:])
            ins.then_inc(coeff_t, 1)

        def c_rows(k, t):
            if t == 0:
                pe.wait_ge(mr_ready, k + 1)
            if not isinstance(k, int) or k * NG + t >= 2:
                pe.wait_ge(cb_out, k * NG + t - 1)
            pe.matmul(PT[:, t % 2, :], MR[:], coeffT[:, t * GT:(t + 1) * GT], start=True, stop=True).then_inc(cb_mm, 1)

        pe.wait_ge(coeff_out, NG)
        for t in range(NG):
            c_rows(0, t)

        def experts(k, last):
            for i in range(HALF):
                pe.wait_ge(w_lo, (k * HALF + EXPERT + i) * 2 + 2)
                for t in range(NG):
                    gate_up(k * HALF + NS + i, (EXPERT + i) % 2, t)
                    if i == HALF - 1 and not last:
                        c_rows(k + 1, t)
        with pe.Fori(0, KB - 1) as k:
            experts(k, False)
        experts(KB - 1, True)

        def down_w(h, c):
            return WB[h][:, DOWN % 2, c, :]

        pe.wait_ge(w_lo, 2 * DOWN + 2)
        pe.wait_ge(cb_out, KB * NG)
        for s in range(2):
            down(2, down_w, d_lo, d_mm, d_out, s, s)
        with pe.Fori(1, NT // 2) as p:
            for s in range(2):
                down(2, down_w, d_lo, d_mm, d_out, p * 2 + s, s)


def build(nc, a, out):
    with ExitStack() as whole:
        X = whole.enter_context(nc.sbuf_tensor("x_rows", [P, NT, HID], F32))
        ident = whole.enter_context(nc.sbuf_tensor("ident", [P, P], F32))
        x1_stats = whole.enter_context(nc.sbuf_tensor("x1_stats", [P, NT, 6], F32))
        with ExitStack() as ctx:
            build_attention(nc, ctx, a, X, ident, x1_stats)
        with ExitStack() as ctx:
            build_ffn(nc, ctx, a, X, ident, x1_stats, out)


def constants():
    p = np.arange(P)
    key = (np.arange(4 * W) // (2 * W) - 1) * W + np.arange(4 * W) % W
    rel = key[None, :] - (p % W)[:, None]
    inside = (rel <= 0) & (rel > -W)
    slope = np.power(np.float32(2.0), np.float32(-8.0) * np.arange(H, dtype=np.float32) / np.float32(H))
    pair = np.arange(2 * HK)
    heads = (pair // 2 * G + pair % 2 * 2)[None, :] + (p // W)[:, None]
    return {
        "identity": np.eye(P, dtype=np.float32),
        "head_rows": (p[:, None] // D == np.arange(HK)[None, :]).astype(np.float32),
        "slopes": (slope[heads] * np.float32(D ** 0.5)).astype(np.float32),
        "rel_pen": np.stack([rel, np.where(inside, 0.0, MASKED)], 1).astype(np.float32),
    }


def kernel(**inputs):
    import concourse.bacc as bacc
    from concourse.bass_utils import run_bass_kernel_spmd

    nc = bacc.Bacc("TRN2", target_bir_lowering=False, num_devices=1)
    arrays, aps = {}, {}
    for name, v in {**inputs, **constants()}.items():
        v = np.ascontiguousarray(v)
        arrays[f"in_{name}"] = v
        aps[name] = nc.dram_tensor(f"in_{name}", v.shape, mybir.dt.from_np(v.dtype), kind="ExternalInput").ap()
    out = nc.dram_tensor("out", (B, T, HID), F32, kind="ExternalOutput").ap()
    build(nc, aps, out)
    return run_bass_kernel_spmd(nc, [arrays], core_ids=[0]).results[0]["out"]
```

```python
from contextlib import ExitStack

import numpy as np

import concourse.bass as bass
from concourse import mybir

ALU = mybir.AluOpType
ACT = mybir.ActivationFunctionType
AX = mybir.AxisListType
F32 = mybir.dt.float32
F32R = mybir.dt.float32r

P = 128
B, T, HID = 8, 256, 512
H, HK = 32, 8
G = H // HK
D = HID // H
W = 64
NB = T // W
HC = HID // P
TB = T // P
NT = B * TB
UNITS = HK * NB
RING = 4
LN_EPS = 1e-5
BANKS = 3
MASKED = -3.0e38
PASSES = (("hi", "hi"), ("lo", "hi"), ("hi", "lo"))

E, TOPK, KB, FI = 128, 4, 8, 256
FS = 512
FFN_EPS = 1e-8
NG = 4
GT = B * T // NG


def wait_alone(eng, sem, value, passed):
    eng.wait_ge(sem, value)
    eng.sem_inc(passed, 1)


def newton_rsqrt(dve, done, count, var_eps, root, rstd, tmp):
    def link(ins):
        count[0] += 1
        ins.then_inc(done, 1)
        dve.wait_ge(done, count[0])
    link(dve.reciprocal(rstd, root))
    link(dve.tensor_tensor(tmp, rstd, rstd, ALU.mult))
    link(dve.tensor_tensor(tmp, tmp, var_eps, ALU.mult))
    link(dve.tensor_scalar(tmp, tmp, -0.5, 1.5, ALU.mult, ALU.add))
    link(dve.tensor_tensor(rstd, rstd, tmp, ALU.mult))


def build_attention(nc, ctx, a, X, ident, x1_mv):
    def sb(name, shape, dt=F32):
        return ctx.enter_context(nc.sbuf_tensor(name, shape, dt))

    def ps(name, shape):
        return ctx.enter_context(nc.psum_tensor(name, shape, F32))

    def sem(name):
        return ctx.enter_context(nc.semaphore(name))

    WQ = {h: sb(f"wq_{h}", [P, 2 * HC, HID], F32R) for h in ("hi", "lo")}
    WKV = {h: sb(f"wkv_{h}", [P, 4, HC, P], F32R) for h in ("hi", "lo")}
    WO = {h: sb(f"wo_{h}", [P, HC, HID], F32R) for h in ("hi", "lo")}
    ctx_rows = sb("ctx_rows", [P, TB, HID])
    xn = sb("xn", [P, TB, HID])
    AT = {h: sb(f"actT_{h}", [P, 2 * HC, T], F32R) for h in ("hi", "lo")}
    Q = {h: sb(f"qT_{h}", [P, 2, NB, 2, W], F32R) for h in ("hi", "lo")}
    K = {h: sb(f"kT_{h}", [P, NB, 2, W], F32R) for h in ("hi", "lo")}
    KM = {h: sb(f"kmask_{h}", [P, 2, NB * 2 * W], F32R) for h in ("hi", "lo")}
    VT = sb("vT", [P, NB, 2, W])
    VA = sb("v_ones", [P, NB, HK, 2 * D])
    bias = sb("bias", [P, HK * 2, 4 * W])
    SC = sb("scores_sb", [P, RING, 2, 4 * W])
    NM = sb("neg_max", [P, RING, 2])
    PT = sb("probsT", [P, 2, 2 * NB, G, W])
    OS = sb("oT_sums", [P, T])
    RI = sb("inv_sums", [P, TB, G])
    O = sb("o_rows", [P, TB, HID])
    OT = {h: sb(f"oT_{h}", [P, TB, HC, P], F32R) for h in ("hi", "lo")}
    stage = PT[:, :, :, :, :].rearrange("p b h r q -> p (b h r q)").rearrange("p (s n) -> p s n", s=4)
    rel_pen = SC[:, 0, :, :]
    head_rows = sb("head_rows", [P, HK])
    slopes = sb("slopes", [P, 2 * HK])
    stats = sb("stats", [P, NT, 6])
    x1_stats, batch_mv = sb("x1_stats", [P, TB, 6]), sb("batch_mean_var", [P, TB, 2])
    mv = sb("mean_var", [P, NT, 2])
    var_eps = sb("var_eps", [P, NT])
    root = sb("root", [P, NT])
    rstd = sb("rstd", [P, NT])
    tmp = sb("tmp", [P, NT])
    gate = sb("gate", [P, 1])
    tg = sb("tanh_gate", [P, 1])

    PJ = ps("ps_proj", [P, 2, HID])
    PS = ps("ps_scores", [P, BANKS, 2, 4 * W])
    PX = ps("ps_probsT", [P, 2, 2, 2, P])
    PON = ps("ps_o", [P, 2, T])
    PO, PN = PON[:, 0, :], PON[:, 1, :]

    consts_in, ident_in, x_in, ctx_in = sem("consts_in"), sem("ident_in"), [sem(f"x_in{n}") for n in range(B)], sem("ctx_in")
    stage_in = [sem(f"stage_in{n}") for n in range(8)]
    weights_hi, chain, root_done, tg_done = sem("weights_hi"), sem("chain"), sem("root_done"), sem("tg_done")
    weights_lo = [sem("weights_lo_pool"), sem("weights_lo_dve")]
    pool_ready, dve_passed = sem("pool_ready"), sem("dve_passed")
    xn_ready, prep_t, prep_hi, prep_lo = sem("xn_ready"), sem("prep_t"), sem("prep_hi"), sem("prep_lo")
    proj_mm, proj_hi, proj_lo = sem("proj_mm"), sem("proj_hi"), sem("proj_lo")
    v_turned, v_ready, km_ready = sem("v_turned"), sem("v_ready"), sem("km_ready")
    scores_mm, sc_done, exp_done, probs_t = sem("scores_mm"), sem("sc_done"), sem("exp_done"), sem("probs_t")
    pt_done = [sem("pt_done_act"), sem("pt_done_dve")]
    pv_mm, oT_out, o_turned, inv_done, o_done = (
        sem("pv_mm"), sem("oT_out"), sem("o_turned"), sem("inv_done"), sem("o_done"))
    oT_mm, oT_hi, oT_lo, wo_mm, x1_done, ve_done, x1_st, x1_ag = (
        sem("oT_mm"), sem("oT_hi"), sem("oT_lo"), sem("wo_mm"), sem("x1_done"), sem("ve_done"), sem("x1_st"),
        sem("x1_ag"))

    x_t = a["x"].rearrange("b (t p) d -> p b t d", p=P)
    ctx_t = a["ctx_2048"].rearrange("b (t p) d -> p b t d", p=P)

    wq_d = a["L0_xattn_Wq"].rearrange("(c p) n -> p c n", p=P)
    wo_d = a["L0_xattn_Wo"].rearrange("(c p) n -> p c n", p=P)
    kv_d = [a[f"L0_xattn_{n}"].rearrange("(c p) n -> p c n", p=P) for n in ("Wsk", "Wk", "Wsv", "Wv")]

    def q_order(part, c):
        return part[:, c, :].rearrange("p (r g d) -> p g r d", r=G, g=HK)

    def kv_half(m):
        return kv_d[m], {h: WKV[h][:, m] for h in WKV}, ("c n", dict(c=HC))

    halves = [kv_half(0), kv_half(1)]
    for c in range(2 * HC):
        halves.append((wq_d[:, c, :], {h: q_order(WQ[h], c) for h in WQ}, ("g r d", dict(g=HK, r=G))))
    halves += [kv_half(2), kv_half(3)]
    for c in range(HC):
        halves.append((wo_d[:, c, :], {h: WO[h][:, c, :] for h in WO}, None))
    FIRST_Q, FIRST_V, FIRST_O = 2, 2 + 2 * HC, 4 + 2 * HC

    def raw(n):
        v = stage[:, (n // 2) % 4, (n % 2) * HID:(n % 2 + 1) * HID]
        shape = halves[n][2]
        return v.rearrange(f"p ({shape[0]}) -> p {shape[0]}", **shape[1]) if shape else v

    def probs_out(eng, nce, b, u):
        g, i = divmod(u, NB)
        if i < 2 and g >= 2:
            eng.wait_ge(pv_mm, b * HK + g - 1)
        eng.wait_ge(probs_t, b * UNITS + u + 1)
        first = 1 if i == 0 else 0
        dst = PT[:, g % 2, 2 * i + first:2 * i + 2].rearrange("p h r q -> p (h r q)")
        src = PX[:, u % 2, first:2].rearrange("p h k q -> p (h k q)")
        if u % 2 == 0:
            nce.activation(dst, src, ACT.Copy).then_inc(pt_done[0], 1)
        else:
            nce.tensor_copy(dst, src).then_inc(pt_done[1], 1)

    def wait_split(eng, n):
        eng.wait_ge(weights_lo[n % 2], n // 2 + 1)

    def split_lo(eng, n):
        eng.wait_ge(weights_hi, n + 1)
        eng.tensor_tensor(halves[n][1]["lo"], raw(n), halves[n][1]["hi"].bitcast(F32),
                          ALU.subtract).then_inc(weights_lo[n % 2], 1)

    def tile_columns(i):
        src, t = i // TB, i % TB
        return slice(None), slice(src * HC, (src + 1) * HC), slice(t * P, (t + 1) * P)

    def row(view, n):
        return view[:, bass.ds(n, 1), :].rearrange("p o d -> p (o d)")

    LN_GROUPS = [(0, TB), (TB, 2 * TB), (2 * TB, NT)]

    TURN, OUT = 2, 3
    PV, PV_OUT, TURN_O, NORM = 7, 8, 9, 10
    PREP = [6, 10, 14, 18]

    block = ctx.enter_context(nc.Block())

    @block.sync
    def _(sp):
        sp.dma_start(ctx_rows[:], ctx_t[:, 0]).then_inc(ctx_in, 16)
        sp.dma_start(ident[:], a["identity"]).then_inc(ident_in, 16)
        sp.dma_start(X[:, 0:TB, :], x_t[:, 0]).then_inc(x_in[0], 16)
        for n in range(len(halves)):
            if n >= 8:
                wait_split(sp, n - 8)
            src = halves[n][0]
            dst = stage[:, (n // 2) % 4, (n % 2) * HID:(n % 2 + 1) * HID]
            if len(src.shape) == 3:
                dst = dst.rearrange("p (c n) -> p c n", c=HC)
            sp.dma_start(dst, src).then_inc(stage_in[n % 8], 16)
            if n == 7:
                for dst, src in ((head_rows[:], a["head_rows"]), (slopes[:], a["slopes"]), (rel_pen, a["rel_pen"]),
                                 (gate[:], a["g_xattn"].partition_broadcast(P))):
                    sp.dma_start(dst, src).then_inc(consts_in, 16)
        for n in range(1, B):
            sp.dma_start(X[:, TB * n:TB * (n + 1), :], x_t[:, n]).then_inc(x_in[n], 16)
        with sp.Fori(0, B - 1) as b:
            sp.wait_ge(prep_t, b * 4 + 2)
            sp.dma_start(ctx_rows[:], ctx_t[:, bass.ds(b + 1, 1)].rearrange("p b t d -> p (b t) d")).then_inc(ctx_in, 16)

    @block.gpsimd
    def _(pool):
        pool.memset(VA[:], 1.0).then_inc(pool_ready, 1)
        for n in range(0, len(halves), 2):
            split_lo(pool, n)
        pool.wait_ge(consts_in, 64)
        with pool.Fori(0, B) as b:
            for g in range(HK):
                if g == 0:
                    pool.wait_ge(proj_lo, b * 5 + 1)
                if g >= 2:
                    pool.wait_ge(scores_mm, b * UNITS + NB * (g - 1))
                for h in ("hi", "lo"):
                    pool.tensor_tensor(KM[h][:, g % 2, :], K[h][:].bitcast(F32).rearrange("p j s w -> p (j s w)"),
                                       head_rows[:, g:g + 1].broadcast_to([P, NB * 2 * W]),
                                       ALU.mult).then_inc(km_ready, 1)

    def probs_out(eng, nce, b, u):
        g, i = divmod(u, NB)
        if i < 2 and g >= 2:
            eng.wait_ge(pv_mm, b * HK + g - 1)
        eng.wait_ge(probs_t, b * UNITS + u + 1)
        first = 1 if i == 0 else 0
        dst = PT[:, g % 2, 2 * i + first:2 * i + 2].rearrange("p h r q -> p (h r q)")
        src = PX[:, u % 2, first:2].rearrange("p h k q -> p (h k q)")
        if u % 2 == 0:
            nce.activation(dst, src, ACT.Copy).then_inc(pt_done[0], 1)
        else:
            nce.tensor_copy(dst, src).then_inc(pt_done[1], 1)

    @block.scalar
    def _(act):
        def split_hi(n):
            act.wait_ge(stage_in[n % 8], 16 * (n // 8) + 16)
            act.activation(halves[n][1]["hi"], raw(n), ACT.Copy).then_inc(weights_hi, 1)

        def prep(b, i):
            act.wait_ge(prep_t, b * 4 + i + 1)
            act.activation(AT["hi"][tile_columns(i)], PJ[:, i % 2, :].rearrange("p (c n) -> p c n", c=HC),
                           ACT.Copy).then_inc(prep_hi, 1)

        def proj_out(b, n):
            act.wait_ge(proj_mm, b * 6 + n + 1)
            if 1 <= n <= G:
                r = n - 1
                act.activation(Q["hi"][:, r // 2, :, r % 2, :],
                               PJ[:, n % 2, 0:T].rearrange("p (i w) -> p i w", i=NB), ACT.Copy).then_inc(proj_hi, 1)
            else:
                dst = K["hi"] if n == 0 else VT
                act.activation(dst[:].rearrange("p j s w -> p s j w"),
                               PJ[:, n % 2, :].rearrange("p (s j w) -> p s j w", s=2, j=NB),
                               ACT.Copy).then_inc(proj_hi, 1)

        def exps(b, s):
            n = 2 * W if s % NB == 0 else 4 * W
            for pp in range(2):
                act.wait_ge(sc_done, b * 2 * UNITS + 2 * s + pp + 1)
                act.activation(SC[:, s % RING, pp, 0:n], SC[:, s % RING, pp, 0:n], ACT.Exp,
                               bias=NM[:, s % RING, pp:pp + 1], scale=-1.0).then_inc(exp_done, 1)

        def pv_out(b, g):
            act.wait_ge(pv_mm, b * HK + g + 1)
            if g >= 1:
                act.wait_ge(o_turned, b * HK + g)
            act.activation(OS[:], PO, ACT.Copy).then_inc(oT_out, 1)

        def oT_high(b, t):
            act.wait_ge(oT_mm, b * TB + t + 1)
            act.activation(OT["hi"][:, t], PX[:, t].rearrange("p h k n -> p (h k) n"), ACT.Copy).then_inc(oT_hi, 1)

        def boundary(b, before, after):
            if before:
                pv_out(b - 1, HK - 2)
            if after:
                proj_out(b, 0)
            if before:
                probs_out(act, nc.scalar, b - 1, UNITS - 2)
            if after:
                proj_out(b, 1)
                proj_out(b, 2)
            if before:
                pv_out(b - 1, HK - 1)
            if after:
                proj_out(b, 3)
                proj_out(b, 4)
            if before:
                for t in range(TB):
                    oT_high(b - 1, t)
            if after:
                proj_out(b, 5)

        def units(b, first, last):
            for s in range(UNITS):
                if s >= OUT and (s - OUT) % 2 == 0:
                    probs_out(act, nc.scalar, b, s - OUT)
                g, r = divmod(s - PV_OUT, NB)
                if r == 0 and g >= 0:
                    pv_out(b, g)
                exps(b, s)
                if first and s == 25:
                    roots(2)
                if not last and s - 1 in PREP:
                    prep(b + 1, PREP.index(s - 1))

        def roots(n):
            act.wait_ge(ve_done, n + 1)
            ts = slice(*LN_GROUPS[n])
            act.activation(root[:, ts], var_eps[:, ts], ACT.Sqrt).then_inc(root_done, 1)

        roots(0)
        prep(0, 0)
        prep(0, 1)
        for n in range(4):
            split_hi(n)
        prep(0, 2)
        prep(0, 3)
        for n in range(4, 12):
            split_hi(n)
        boundary(0, False, True)
        for n in range(12, len(halves)):
            split_hi(n)
        roots(1)
        act.wait_ge(consts_in, 64)
        act.activation(tg[:], gate[:], ACT.Tanh).then_inc(tg_done, 1)
        units(0, True, False)
        with act.Fori(1, B - 1) as b:
            boundary(b, True, True)
            units(b, False, False)
        boundary(B - 1, True, True)
        units(B - 1, False, True)
        boundary(B, True, False)

    @block.vector
    def _(dve):
        count = [0]

        def link(ins):
            count[0] += 1
            ins.then_inc(chain, 1)
            dve.wait_ge(chain, count[0])

        def one_row_stats(t):
            dve.wait_ge(x_in[t // TB], 16)
            link(dve.bn_stats(stats[:, t, :], X[:, t, :]))
            link(dve.bn_aggr(mv[:, t, :], stats[:, t, :]))

        def variances(first, last):
            ts = slice(first, last)
            dve.tensor_scalar(var_eps[:, ts], mv[:, ts, 1], LN_EPS, None, ALU.add).then_inc(ve_done, 1)

        def inverse_roots(first, last):
            dve.wait_ge(root_done, LN_GROUPS.index((first, last)) + 1)
            ts = slice(first, last)
            newton_rsqrt(dve, chain, count, var_eps[:, ts], root[:, ts], rstd[:, ts], tmp[:, ts])

        def normalise(b, t):
            one = bass.ds(b * TB + t, 1)
            dve.tensor_scalar(xn[:, t, :], row(X, b * TB + t), mv[:, one, 0], rstd[:, one],
                              ALU.subtract, ALU.mult).then_inc(xn_ready, 1)

        def prep(b, i):
            dve.wait_ge(prep_hi, b * 4 + i + 1)
            dve.tensor_tensor(AT["lo"][tile_columns(i)], PJ[:, i % 2, :].rearrange("p (c n) -> p c n", c=HC),
                              AT["hi"][tile_columns(i)].bitcast(F32), ALU.subtract).then_inc(prep_lo, 1)

        def proj_out(b, n):
            dve.wait_ge(proj_hi, b * 6 + n + 1)
            if 1 <= n <= G:
                r = n - 1
                dve.tensor_tensor(Q["lo"][:, r // 2, :, r % 2, :],
                                  PJ[:, n % 2, 0:T].rearrange("p (i w) -> p i w", i=NB),
                                  Q["hi"][:, r // 2, :, r % 2, :].bitcast(F32), ALU.subtract).then_inc(proj_lo, 1)
            else:
                dve.tensor_tensor(K["lo"][:].rearrange("p j s w -> p s j w"),
                                  PJ[:, n % 2, :].rearrange("p (s j w) -> p s j w", s=2, j=NB),
                                  K["hi"][:].bitcast(F32).rearrange("p j s w -> p s j w"),
                                  ALU.subtract).then_inc(proj_lo, 1)

        def maxima(b, s):
            g, i = divmod(s, NB)
            n = 2 * W if i == 0 else 4 * W
            if s >= RING:
                dve.wait_ge(probs_t, b * UNITS + s - RING + 1)
            wait_alone(dve, scores_mm, b * UNITS + s + 1, dve_passed)
            for pp in range(2):
                dve.tensor_tensor_reduce(SC[:, s % RING, pp, 0:n], PS[:, s % BANKS, pp, 0:n],
                                         bias[:, 2 * g + pp, 4 * W - n:4 * W], -float(D) ** -0.5, 3e38,
                                         ALU.add, ALU.min, NM[:, s % RING, pp:pp + 1]).then_inc(sc_done, 1)

        def norm(b, g):
            dve.wait_ge(o_turned, b * HK + g + 1)
            v = PN.rearrange("p (t r e) -> p t r e", t=TB, r=G)
            dve.reciprocal(RI[:], v[:, :, :, D]).then_inc(inv_done, 1)
            dve.wait_ge(inv_done, b * HK + g + 1)
            dve.tensor_tensor(O[:, :, g * G * D:(g + 1) * G * D].rearrange("p t (r d) -> p t r d", r=G),
                              v[:, :, :, 0:D], RI[:].unsqueeze(3).broadcast_to([P, TB, G, D]),
                              ALU.mult).then_inc(o_done, 1)

        def oT_low(b, t):
            dve.wait_ge(oT_hi, b * TB + t + 1)
            dve.tensor_tensor(OT["lo"][:, t], PX[:, t].rearrange("p h k n -> p (h k) n"),
                              OT["hi"][:, t].bitcast(F32), ALU.subtract).then_inc(oT_lo, 1)

        def residual(b, t):
            x1 = row(X, b * TB + t)
            dve.wait_ge(wo_mm, b * TB + t + 1)
            dve.scalar_tensor_tensor(out=x1, in0=PS[:, t].rearrange("p k n -> p (k n)"), scalar=tg[:, 0:1],
                                     in1=x1, op0=ALU.mult, op1=ALU.add).then_inc(x1_done, 1)
            wait_alone(dve, x1_done, b * TB + t + 1, dve_passed)
            dve.bn_stats(x1_stats[:, t, :], x1).then_inc(x1_st, 1)
            wait_alone(dve, x1_st, b * TB + t + 1, dve_passed)
            dve.bn_aggr(batch_mv[:, t, :], x1_stats[:, t, :]).then_inc(x1_ag, 1)
            dve.wait_ge(x1_ag, b * TB + t + 1)
            dve.tensor_copy(row(x1_mv, b * TB + t), batch_mv[:, t, :])

        def boundary(b, before, after):
            if before:
                probs_out(dve, nc.vector, b - 1, UNITS - 3)
            if after:
                proj_out(b, 0)
            if before:
                norm(b - 1, HK - 2)
            if after:
                proj_out(b, 1)
            if before:
                probs_out(dve, nc.vector, b - 1, UNITS - 1)
            if after:
                proj_out(b, 2)
                proj_out(b, 3)
            if before:
                norm(b - 1, HK - 1)
            if after:
                proj_out(b, 4)
            if before:
                for t in range(TB):
                    oT_low(b - 1, t)
                for t in range(TB):
                    residual(b - 1, t)
            if after:
                dve.wait_ge(v_turned, b + 1)
                dve.tensor_copy(VA[:, :, :, 0:D], PJ[:, 0, :].rearrange("p (j g d) -> p j g d", j=NB, g=HK)
                                ).then_inc(v_ready, 1)

        def units(b, first, last):
            for s in range(UNITS):
                if s >= OUT and (s - OUT) % 2 == 1:
                    probs_out(dve, nc.vector, b, s - OUT)
                g, r = divmod(s - NORM, NB)
                if r == 0 and g >= 0:
                    norm(b, g)
                maxima(b, s)
                if first and 12 <= s < 12 + NT - 2 * TB:
                    one_row_stats(s - 12 + 2 * TB)
                if first and s == 24:
                    variances(*LN_GROUPS[2])
                if first and s == 27:
                    inverse_roots(*LN_GROUPS[2])
                if not last:
                    if 9 <= s < 9 + TB:
                        normalise(b + 1, s - 9)
                    if s - 2 in PREP:
                        prep(b + 1, PREP.index(s - 2))

        for t in range(TB):
            one_row_stats(t)
        variances(*LN_GROUPS[0])
        inverse_roots(*LN_GROUPS[0])
        for t in range(TB):
            normalise(0, t)
        prep(0, 0)
        prep(0, 1)
        split_lo(dve, 1)
        split_lo(dve, 3)
        prep(0, 2)
        prep(0, 3)
        for n in range(5, 12, 2):
            split_lo(dve, n)
        dve.wait_ge(consts_in, 64)
        for k in range(2 * HK):
            ins = dve.scalar_tensor_tensor(out=bias[:, k, :], in0=rel_pen[:, 0, :], scalar=slopes[:, k:k + 1],
                                           in1=rel_pen[:, 1, :], op0=ALU.mult, op1=ALU.add)
        link(ins)
        boundary(0, False, True)
        for n in range(13, len(halves), 2):
            split_lo(dve, n)
        for t in range(TB, 2 * TB):
            one_row_stats(t)
        variances(*LN_GROUPS[1])
        inverse_roots(*LN_GROUPS[1])
        dve.wait_ge(pool_ready, 1)
        dve.wait_ge(tg_done, 1)
        units(0, True, False)
        with dve.Fori(1, B - 1) as b:
            boundary(b, True, True)
            units(b, False, False)
        boundary(B - 1, True, True)
        units(B - 1, False, True)
        boundary(B, True, False)

    @block.tensor
    def _(pe):
        def product(out, stat, mov, chunks, before=None):
            for c in chunks:
                if before:
                    before(c)
                for j, (s, m) in enumerate(PASSES):
                    ins = pe.matmul(out, stat(s, c), mov(m, c), start=c == chunks[0] and j == 0,
                                    stop=c == chunks[-1] and j == 2)
            return ins

        def prep(b, i):
            src, t = i // TB, i % TB
            if src == 0:
                pe.wait_ge(ctx_in, b * 16 + 16)
            else:
                pe.wait_ge(xn_ready, b * TB + t + 1)
            if i >= 2:
                pe.wait_ge(prep_lo, b * 4 + i - 1)
            rows = ctx_rows if src == 0 else xn
            for c in range(HC):
                ins = pe.transpose(PJ[:, i % 2, c * P:(c + 1) * P], rows[:, t, c * P:(c + 1) * P], ident[:])
            ins.then_inc(prep_t, 1)

        def proj(b, n, first):
            if n == 0:
                pe.wait_ge(prep_lo, b * 4 + 4)
            if n >= 2:
                pe.wait_ge(proj_lo, b * 5 + n - 1)
            if 1 <= n <= G:
                ins = product(PJ[:, n % 2, 0:T], lambda h, c: WQ[h][:, c, (n - 1) * P:n * P],
                              lambda h, c: AT[h][:, c, :], range(2 * HC),
                              (lambda c: wait_split(pe, FIRST_Q + c)) if first and n == 1 else None)
            else:
                m = 0 if n == 0 else 2
                for src in range(2):
                    if first:
                        wait_split(pe, (0 if n == 0 else FIRST_V) + src)
                    ins = product(PJ[:, n % 2, src * T:(src + 1) * T], lambda h, c: WKV[h][:, m + src, c, :],
                                  lambda h, c: AT[h][:, src * HC + c, :], range(HC))
            ins.then_inc(proj_mm, 1)

        def turn_v(b):
            pe.wait_ge(proj_hi, b * 6 + 6)
            pe.wait_ge(proj_lo, b * 5 + 5)
            for j in range(NB):
                ins = pe.transpose(PJ[:, 0, j * P:(j + 1) * P], VT[:, j].rearrange("p s w -> p (s w)"), ident[:])
            ins.then_inc(v_turned, 1)

        def score(b, s, first):
            g, i = divmod(s, NB)
            n = 2 * W if i == 0 else 4 * W
            if i == 0:
                pe.wait_ge(km_ready, b * 2 * HK + 2 * (g + 1))
            if s >= BANKS:
                pe.wait_ge(sc_done, b * 2 * UNITS + 2 * (s - BANKS + 1))
            elif s < TB and not first:
                pe.wait_ge(x1_done, (b - 1) * TB + s + 1)
            for pp in range(2):
                for j, (sp_, mp) in enumerate(PASSES):
                    ins = pe.matmul(PS[:, s % BANKS, pp, 0:n], Q[sp_][:, pp, i].rearrange("p r w -> p (r w)"),
                                    KM[mp][:, g % 2, (i + 1) * 2 * W - n:(i + 1) * 2 * W],
                                    start=j == 0, stop=j == 2)
            ins.then_inc(scores_mm, 1)

        def turn_probs(b, u):
            g, i = divmod(u, NB)
            pe.wait_ge(exp_done, b * 2 * UNITS + 2 * u + 2)
            if u >= 2:
                pe.wait_ge(pt_done[u % 2], b * UNITS // 2 + u // 2)
            first = 1 if i == 0 else 0
            for h in range(first, 2):
                for pp in range(2):
                    ins = pe.transpose(PX[:, u % 2, h, pp, :], SC[:, u % RING, pp, (h - first) * P:(h - first + 1) * P],
                                       ident[:])
            ins.then_inc(probs_t, 1)

        def times_v(b, g):
            if g == 0:
                pe.wait_ge(v_ready, b + 1)
            for e in range(2):
                pe.wait_ge(pt_done[e], b * UNITS // 2 + 2 * (g + 1))
            if g >= 1:
                pe.wait_ge(o_done, b * HK + g)
            for j in range(NB):
                n = min(2 * W, T - j * W)
                for r in range(G):
                    ins = pe.matmul(PO[32 * r:32 * r + 2 * D, j * W:j * W + n], VA[:, j, g, :],
                                    PT[:, g % 2, 2 * j + 1:2 * j + 1 + n // W, r, :],
                                    start=j == 0, stop=j == NB - 1, skip_group_check=True)
            ins.then_inc(pv_mm, 1)

        def turn_o(b, g):
            pe.wait_ge(oT_out, b * HK + g + 1)
            for t in range(TB):
                ins = pe.transpose(PN[:, t * P:(t + 1) * P], OS[:, t * P:(t + 1) * P], ident[:])
            ins.then_inc(o_turned, 1)

        def boundary(b, before, after):
            first = not before
            if after:
                proj(b, 0, first)
            if before:
                turn_probs(b - 1, UNITS - 2)
                turn_o(b - 1, HK - 2)
            if after:
                proj(b, 1, first)
            if before:
                turn_probs(b - 1, UNITS - 1)
            if after:
                proj(b, 2, first)
            if before:
                times_v(b - 1, HK - 1)
            if after:
                proj(b, 3, first)
            if before:
                turn_o(b - 1, HK - 1)
            if after:
                proj(b, 4, first)
            if before:
                pe.wait_ge(o_done, (b - 1) * HK + HK)
                for t in range(TB):
                    for c in range(HC):
                        ins = pe.transpose(PX[:, t].rearrange("p h k n -> p (h k) n")[:, c, :],
                                           O[:, t, c * P:(c + 1) * P], ident[:])
                    ins.then_inc(oT_mm, 1)
            if after:
                proj(b, 5, first)
            if before:
                for t in range(TB):
                    pe.wait_ge(oT_lo, (b - 1) * TB + t + 1)
                    product(PS[:, t].rearrange("p k n -> p (k n)"), lambda h, c: OT[h][:, t, c, :],
                            lambda h, c: WO[h][:, c, :], range(HC)).then_inc(wo_mm, 1)
            if after:
                turn_v(b)

        def units(b, first, last):
            for s in range(UNITS):
                score(b, s, first)
                if s >= TURN:
                    turn_probs(b, s - TURN)
                g, r = divmod(s - PV, NB)
                if r == 0 and g >= 0:
                    times_v(b, g)
                g, r = divmod(s - TURN_O, NB)
                if r == 0 and g >= 0:
                    turn_o(b, g)
                if not last and s in PREP:
                    if s == PREP[0]:
                        pe.wait_ge(v_ready, b + 1)
                    prep(b + 1, PREP.index(s))

        pe.wait_ge(ident_in, 16)
        for i in range(4):
            prep(0, i)
        boundary(0, False, True)
        units(0, True, False)
        for n in range(FIRST_O, len(halves)):
            wait_split(pe, n)
        with pe.Fori(1, B - 1) as b:
            boundary(b, True, True)
            units(b, False, False)
        boundary(B - 1, True, True)
        units(B - 1, False, True)
        boundary(B, True, False)


def build_ffn(nc, ctx, a, X, ident, x1_mv, out):
    def sb(name, shape, dt=F32):
        return ctx.enter_context(nc.sbuf_tensor(name, shape, dt))

    def ps(name, shape):
        return ctx.enter_context(nc.psum_tensor(name, shape, F32))

    def sem(name):
        return ctx.enter_context(nc.semaphore(name))

    TOK = B * T
    XT = {h: sb(f"xnT_{h}", [P, HC, TOK], F32R) for h in ("hi", "lo")}
    big = sb("big", [P, 4, TOK])
    hT = big[:, :, :]
    mixed, cB = big[:, 0:2, :], big[:, 2, :]
    WB = {h: sb(f"w_{h}", [P, 2, 2, 4 * P], F32R) for h in ("hi", "lo")}
    WD = {h: sb(f"w_down_{h}", [P, 4, HID], F32R) for h in ("hi", "lo")}
    raw = sb("w_raw", [P, 2, 2, 4 * P])
    DL = {h: sb(f"down_{h}", [P, 2, 4, P], F32R) for h in ("hi", "lo")}
    PR_ = sb("probs", [P, NT, E + 4])
    left = sb("probs_left", [P, NT * (E + 4)])
    probs_left = left[:, :].rearrange("p (t e) -> p t e", t=NT)
    coeffT = left[:, 0:TOK]
    SG = sb("silu_gate", [P, 2, GT])
    BS = sb("basis", [P, 2, GT])
    xn, logitsT = BS, SG
    MR = sb("mix_column", [P, P])
    amp = sb("amp", [P, KB, 2])
    amp2 = sb("amp2", [P, KB])
    mix = sb("mix", [P, KB])
    escale = sb("escale", [P, 1])
    col = {n: sb(n, [P, 1]) for n in ("mix_sum", "gate_f", "tanh_gate_f")}
    mv = x1_mv
    ln = {n: sb(n, [P, NT]) for n in ("var_eps1", "root1", "rstd1", "tmp1")}
    top8 = sb("top8", [P, NT, 8])
    per_tile = {n: sb(n, [P, NT]) for n in ("row_max", "row_sum", "row_inv", "top_sum", "top_inv")}

    PT = ps("ps_turn", [P, 2, GT])
    PG = ps("ps_gate", [P, 2, GT])
    PU = ps("ps_up", [P, 2, GT])

    consts_in, chain, root_done, tg_done = sem("f_consts"), sem("f_chain"), sem("f_root"), sem("f_tg")
    ve_done, ready = sem("f_var"), sem("f_ready")
    raw_in = [sem("raw_in0"), sem("raw_in1")]
    w_hi, w_lo = sem("w_hi_done"), sem("w_lo_done")
    xn_ready, xn_t, xT_hi, xT_lo = sem("f_xn"), sem("f_xnT"), sem("f_xT_hi"), sem("f_xT_lo")
    router_mm, logits_out, logits_t, logits_in = sem("router_mm"), sem("logits_out"), sem("logits_t"), sem("logits_in")
    shifted, exp_done, coeff_done, coeff_t, coeff_out = (
        sem("shifted"), sem("f_exp"), sem("coeff_done"), sem("coeff_t"), sem("coeff_out"))
    gate_mm, up_mm, silu_done, prod_done, basis_done, acc_done = (
        sem("gate_mm"), sem("up_mm"), sem("silu_done"), sem("prod_done"), sem("basis_done"), sem("acc_done"))
    mr_ready, cb_mm, cb_out = sem("mr_ready"), sem("cb_mm"), sem("cb_out")
    sd_hi, sd_lo, sd_mm, sd_out = sem("sd_hi"), sem("sd_lo"), sem("sd_mm"), sem("sd_out")
    d_hi, d_lo, d_mm, d_out, stored = sem("d_hi"), sem("d_lo"), sem("d_mm"), sem("d_out"), sem("stored")

    NS, NE = FS // P, KB * FI // P
    SHARED, SDOWN, EXPERT = 1, 1 + NS, 3 + NS
    DOWN = EXPERT + NE
    HALF = FI // P

    def cols(w, n):
        return w.rearrange("(c p) n -> p c n", p=P)[:, :, bass.ds(n * P, P)]

    block = ctx.enter_context(nc.Block())

    @block.sync
    def _(sp):
        for dst, src in ((amp[:], a["L0_ffn_amplitudes"]), (escale[:], a["L0_ffn_expert_scale"].rearrange("(e o) -> e o", o=1)),
                         (col["gate_f"][:], a["g_ffn"].partition_broadcast(P))):
            sp.dma_start(dst, src).then_inc(consts_in, 16)

        def load(idx, slot, first, second):
            if not isinstance(idx, int) or idx >= 2:
                sp.wait_ge(w_lo, (idx - 1) * 2)
            sp.dma_start(raw[:, slot, 0, :].rearrange("p (c n) -> p c n", c=first.shape[1])
                         if first.shape[1] * first.shape[2] == 4 * P else
                         raw[:, slot, 0, 0:2 * P].rearrange("p (c n) -> p c n", c=2), first).then_inc(raw_in[slot], 16)
            sp.dma_start(raw[:, slot, 1, :].rearrange("p (c n) -> p c n", c=second.shape[1])
                         if second.shape[1] * second.shape[2] == 4 * P else
                         raw[:, slot, 0, 2 * P:4 * P].rearrange("p (c n) -> p c n", c=2), second).then_inc(raw_in[slot], 16)

        router = cols(a["L0_ffn_w_router"], 0)
        load(0, 0, router[:, 0:2], router[:, 2:4])
        for n in range(NS):
            load(SHARED + n, (SHARED + n) % 2, cols(a["L0_ffn_shared_w_gate"], n), cols(a["L0_ffn_shared_w_up"], n))
        sdown = a["L0_ffn_shared_w_down"].rearrange("(c p) n -> p c n", p=P)
        for n in range(2):
            load(SDOWN + n, (SDOWN + n) % 2, sdown[:, 2 * n:2 * n + 1], sdown[:, 2 * n + 1:2 * n + 2])
        with sp.Fori(0, KB) as k:
            for i in range(HALF):
                load(k * HALF + EXPERT + i, (EXPERT + i) % 2, cols(a["L0_ffn_w_gate"], k * HALF + i),
                     cols(a["L0_ffn_w_up"], k * HALF + i))
        down = a["L0_ffn_w_down"].rearrange("(c p) n -> p c n", p=P)
        load(DOWN, DOWN % 2, down[:, 0:1], down[:, 1:2])
        out_t = out.rearrange("b (t p) d -> p (b t) d", p=P)
        with sp.Fori(0, NT) as t:
            sp.wait_ge(d_out, t + 1)
            sp.dma_start(out_t[:, bass.ds(t, 1)], X[:, bass.ds(t, 1), :]).then_inc(stored, 16)
        sp.wait_ge(stored, 16 * NT)

    def place(part, idx, slot):
        if isinstance(idx, int) and (SDOWN <= idx < EXPERT or idx == DOWN):
            c = 2 * (idx - SDOWN) if idx < DOWN else 0
            return WD[part][:, c:c + 2, :]
        return WB[part][:, slot]

    def at_tile(view, t):
        return view[:, :, bass.ds(t * P, P)]

    @block.gpsimd
    def _(pool):
        pool.memset(PR_[:, :, E:E + 4], -5.0).then_inc(ready, 1)

        def split_lo(idx, slot, width=4 * P):
            pool.wait_ge(w_hi, idx * 2 + 2)
            for half in range(2):
                h, lo = (half, 0) if width == 4 * P else (0, half * width)
                where = (slice(None), h, slice(lo, lo + width))
                pool.tensor_tensor(place("lo", idx, slot)[where], raw[:, slot][where],
                                   place("hi", idx, slot)[where].bitcast(F32), ALU.subtract).then_inc(w_lo, 1)
        split_lo(0, 0, 2 * P)
        for idx in range(1, EXPERT + 1):
            split_lo(idx, idx % 2)
        pool.wait_ge(sd_hi, NT)
        pool.wait_ge(sd_lo, NT)
        pool.memset(mixed, 0.0).then_inc(ready, 1)
        pool.wait_ge(ready, 2)

        def add_up(e, i):
            for t in range(NG):
                pool.wait_ge(basis_done, e * NG + t + 1)
                dst = mixed[:, i, t * GT:(t + 1) * GT]
                pool.tensor_tensor(dst, dst, BS[:, t % 2, :], ALU.add).then_inc(acc_done, 1)

        def experts(k):
            for i in range(HALF):
                split_lo(k * HALF + EXPERT + 1 + i, (EXPERT + 1 + i) % 2)
                add_up(k * HALF + i, i)

        with pool.Fori(0, KB - 1) as k:
            experts(k)
        experts(KB - 1)

    @block.scalar
    def _(act):
        def split_hi(idx, slot, used=None, width=4 * P):
            act.wait_ge(raw_in[slot], (idx - slot) * 16 + 32)
            if used:
                act.wait_ge(*used)
            for half in range(2):
                h, lo = (half, 0) if width == 4 * P else (0, half * width)
                where = (slice(None), h, slice(lo, lo + width))
                act.activation(place("hi", idx, slot)[where], raw[:, slot][where], ACT.Copy).then_inc(w_hi, 1)

        act.wait_ge(ve_done, 1)
        act.activation(ln["root1"][:], ln["var_eps1"][:], ACT.Sqrt).then_inc(root_done, 1)
        act.wait_ge(consts_in, 48)
        act.activation(col["tanh_gate_f"][:], col["gate_f"][:], ACT.Tanh).then_inc(tg_done, 1)
        split_hi(0, 0, width=2 * P)
        split_hi(1, 1)
        with act.Fori(0, NT // 2) as p:
            for s in range(2):
                act.wait_ge(xn_t, p * 2 + s + 1)
                act.activation(at_tile(XT["hi"], p * 2 + s), PT[:, s, :].rearrange("p (c n) -> p c n", c=HC),
                               ACT.Copy).then_inc(xT_hi, 1)
        for q in range(NG):
            act.wait_ge(router_mm, q + 1)
            if q >= 2:
                act.wait_ge(logits_t, q - 1)
            act.activation(logitsT[:, q % 2, :], PG[:, q % 2, :], ACT.Copy).then_inc(logits_out, 1)

        def silu(n, t):
            q = n * NG + t
            act.wait_ge(gate_mm, q + 1)
            if not isinstance(q, int) or q >= 2:
                act.wait_ge(prod_done, q - 1)
            act.activation(SG[:, t % 2, :], PG[:, t % 2, :], ACT.Silu).then_inc(silu_done, 1)

        for n in range(NS):
            for t in range(NG):
                if n == 0 and t == 0:
                    act.wait_ge(logits_t, NG)
                silu(n, t)
                if t == 1 and n < NS - 1:
                    split_hi(SHARED + n + 1, (SHARED + n + 1) % 2,
                             (router_mm, NG) if n == 0 else (up_mm, n * NG))
                if n == NS - 1 and t < 2:
                    split_hi(SDOWN + t, (SDOWN + t) % 2)
                if n == NS - 1 and t == 2:
                    split_hi(EXPERT, EXPERT % 2, (up_mm, (NS - 1) * NG))
                if n == 0 and t == NG - 1:
                    act.wait_ge(shifted, 1)
                    act.activation(PR_[:, :, 0:E], PR_[:, :, 0:E], ACT.Exp).then_inc(exp_done, 1)
        for q in range(NG):
            act.wait_ge(coeff_t, q + 1)
            act.activation(coeffT[:, q * GT:(q + 1) * GT], PT[:, q % 2, :], ACT.Copy).then_inc(coeff_out, 1)

        def split_rows(src, chunks, done, mm, t, s):
            if not isinstance(t, int) or t >= 2:
                act.wait_ge(mm, t - 1)
            act.activation(DL["hi"][:, s, 0:chunks, :], at_tile(src, t), ACT.Copy).then_inc(done, 1)

        def split_all(src, chunks, done, mm, rows, before):
            act.wait_ge(rows, before + 1)
            for t in range(4):
                split_rows(src, chunks, done, mm, t, t % 2)
            with act.Fori(1, NG) as q:
                act.wait_ge(rows, q + (before + 1))
                for t in range(4):
                    split_rows(src, chunks, done, mm, q * 4 + t, t % 2)

        split_all(hT, 4, sd_hi, sd_mm, prod_done, (NS - 1) * NG)
        def c_out(k, t):
            act.wait_ge(cb_mm, k * NG + t + 1)
            if not isinstance(k, int) or k >= 1:
                act.wait_ge(basis_done, (k - 1) * HALF * NG + (HALF - 1) * NG + t + 1)
            act.activation(cB[:, t * GT:(t + 1) * GT], PT[:, t % 2, :], ACT.Copy).then_inc(cb_out, 1)

        act.wait_ge(sd_hi, NT)
        act.wait_ge(sd_lo, NT)
        for t in range(NG):
            c_out(0, t)

        def experts(k, last):
            for i in range(HALF):
                for t in range(NG):
                    silu(k * HALF + NS + i, t)
                    if t == 1:
                        if last and i == HALF - 1:
                            split_hi(DOWN, DOWN % 2, (sd_mm, NT))
                        else:
                            split_hi(k * HALF + EXPERT + i + 1, (EXPERT + i + 1) % 2,
                                     (up_mm, (k * HALF + NS + i) * NG))
                    if i == HALF - 1 and not last:
                        c_out(k + 1, t)
        with act.Fori(0, KB - 1) as k:
            experts(k, False)
        experts(KB - 1, True)
        split_all(mixed, 2, d_hi, d_mm, acc_done, (NE - 1) * NG)

    @block.vector
    def _(dve):
        count = [0]

        def link(ins):
            count[0] += 1
            ins.then_inc(chain, 1)
            dve.wait_ge(chain, count[0])

        dve.tensor_scalar(ln["var_eps1"][:], mv[:, :, 1], LN_EPS, None, ALU.add).then_inc(ve_done, 1)
        dve.wait_ge(root_done, 1)
        newton_rsqrt(dve, chain, count, ln["var_eps1"][:], ln["root1"][:], ln["rstd1"][:], ln["tmp1"][:])

        def normalise(t, s):
            one = bass.ds(t, 1)
            dve.tensor_scalar(xn[:, s, :], X[:, one, :].rearrange("p o d -> p (o d)"), mv[:, one, 0],
                              ln["rstd1"][:, one], ALU.subtract, ALU.mult).then_inc(xn_ready, 1)

        def turned_low(t, s):
            dve.wait_ge(xT_hi, t + 1)
            dve.tensor_tensor(at_tile(XT["lo"], t), PT[:, s, :].rearrange("p (c n) -> p c n", c=HC),
                              at_tile(XT["hi"], t).bitcast(F32), ALU.subtract).then_inc(xT_lo, 1)

        for s in range(2):
            normalise(s, s)
        with dve.Fori(0, NT // 2 - 1) as p:
            for s in range(2):
                dve.wait_ge(xn_t, p * 2 + s + 1)
                normalise(p * 2 + s + 2, s)
                turned_low(p * 2 + s, s)
        for s in range(2):
            turned_low(NT - 2 + s, s)
        dve.wait_ge(consts_in, 48)
        link(dve.tensor_tensor(amp[:], amp[:], amp[:], ALU.mult))
        link(dve.tensor_tensor(amp2[:], amp[:, :, 0], amp[:, :, 1], ALU.add))
        link(dve.tensor_reduce(col["mix_sum"][:], amp2[:], AX.X, ALU.add))
        link(dve.tensor_scalar(col["mix_sum"][:], col["mix_sum"][:], FFN_EPS, None, ALU.add))
        link(dve.reciprocal(col["mix_sum"][:], col["mix_sum"][:]))
        link(dve.tensor_scalar(mix[:], amp2[:], col["mix_sum"][:, 0:1], escale[:, 0:1], ALU.mult, ALU.mult))
        dve.wait_ge(ready, 1)
        for q in range(NG):
            dve.wait_ge(logits_t, q + 1)
            dve.tensor_copy(PR_[:, q * 4:(q + 1) * 4, 0:E], PT[:, q % 2, :].rearrange("p (t e) -> p t e", e=E)
                            ).then_inc(logits_in, 1)

        def times(n, t, dst):
            q = n * NG + t
            dve.wait_ge(silu_done, q + 1)
            dve.wait_ge(up_mm, q + 1)
            return dve.tensor_tensor(dst, PU[:, t % 2, :], SG[:, t % 2, :], ALU.mult).then_inc(prod_done, 1)

        probs = PR_[:, :, 0:E]

        def over(v):
            return v.unsqueeze(2).broadcast_to([P, NT, E])

        def top_experts(step):
            w = per_tile
            if step == 0:
                dve.wait_ge(logits_in, NG)
                link(dve.tensor_reduce(w["row_max"][:], probs, AX.X, ALU.max))
            elif step == 1:
                dve.tensor_tensor(probs, probs, over(w["row_max"][:]), ALU.subtract).then_inc(shifted, 1)
            elif step == 4:
                dve.wait_ge(exp_done, 1)
                link(dve.tensor_reduce(w["row_sum"][:], probs, AX.X, ALU.add))
                link(dve.reciprocal(w["row_inv"][:], w["row_sum"][:]))
            elif step == 5:
                link(dve.tensor_tensor(probs, probs, over(w["row_inv"][:]), ALU.mult))
            elif step in (6, 7):
                for t in range((step - 6) * 8, (step - 5) * 8):
                    ins = dve.max(top8[:, t, :], PR_[:, t, 0:E])
                link(ins)
            elif step == 8:
                link(dve.tensor_reduce(w["top_sum"][:], top8[:, :, 0:TOPK], AX.X, ALU.add))
                link(dve.tensor_scalar(w["top_sum"][:], w["top_sum"][:], FFN_EPS, None, ALU.add))
                link(dve.reciprocal(w["top_inv"][:], w["top_sum"][:]))
                link(dve.memset(top8[:, :, TOPK:8], -5.0))
            elif step in (9, 10):
                for t in range((step - 9) * 8, (step - 8) * 8):
                    ins = dve.match_replace(probs_left[:, t, :], top8[:, t, :], PR_[:, t, :], 0.0)
                link(ins)
            elif step == 11:
                link(dve.tensor_tensor(probs, probs, probs_left[:, :, 0:E], ALU.subtract))
            elif step == 12:
                dve.tensor_tensor(probs, probs, over(w["top_inv"][:]), ALU.mult).then_inc(coeff_done, 1)

        for n in range(NS):
            for t in range(NG):
                times(n, t, hT[:, n, t * GT:(t + 1) * GT])
                top_experts(n * NG + t)
        dve.wait_ge(tg_done, 1)

        def rest_rows(src, chunks, hi, lo, t, s):
            dve.wait_ge(hi, t + 1)
            dve.tensor_tensor(DL["lo"][:, s, 0:chunks, :], at_tile(src, t), DL["hi"][:, s, 0:chunks, :].bitcast(F32),
                              ALU.subtract).then_inc(lo, 1)

        def add_rows(mm, done, t, s):
            row = X[:, bass.ds(t, 1), :].rearrange("p o d -> p (o d)")
            dve.wait_ge(mm, t + 1)
            dve.scalar_tensor_tensor(out=row, in0=PT[:, s, :], scalar=col["tanh_gate_f"][:, 0:1], in1=row,
                                     op0=ALU.mult, op1=ALU.add).then_inc(done, 1)

        def down(src, chunks, hi, lo, mm, done):
            for s in range(2):
                rest_rows(src, chunks, hi, lo, s, s)
            with dve.Fori(1, NT // 2) as p:
                for s in range(2):
                    add_rows(mm, done, p * 2 + s - 2, s)
                    rest_rows(src, chunks, hi, lo, p * 2 + s, s)
            for s in range(2):
                add_rows(mm, done, NT - 2 + s, s)

        down(hT, 4, sd_hi, sd_lo, sd_mm, sd_out)

        def mix_column(k):
            if not isinstance(k, int) or k >= 1:
                dve.wait_ge(cb_mm, k * NG)
            dve.tensor_copy(MR[:], mix[:, bass.ds(k, 1)].broadcast_to([P, P])).then_inc(mr_ready, 1)

        mix_column(0)

        def experts(k, last):
            for i in range(HALF):
                for t in range(NG):
                    e = k * HALF + i
                    q = e * NG + t
                    if not isinstance(q, int) or q >= 2:
                        dve.wait_ge(acc_done, q - 1)
                    times(e + NS, t, BS[:, t % 2, :])
                    if i == 0:
                        dve.wait_ge(cb_out, k * NG + t + 1)
                    dve.wait_ge(prod_done, (e + NS) * NG + t + 1)
                    dve.tensor_tensor(BS[:, t % 2, :], BS[:, t % 2, :], cB[:, t * GT:(t + 1) * GT],
                                      ALU.mult).then_inc(basis_done, 1)
                if i == 0 and not last:
                    mix_column(k + 1)
        experts(0, False)
        with dve.Fori(1, KB - 1) as k:
            experts(k, False)
        experts(KB - 1, True)
        down(mixed, 2, d_hi, d_lo, d_mm, d_out)

    @block.tensor
    def _(pe):
        def turn_rows(t, s):
            pe.wait_ge(xn_ready, t + 1)
            if not isinstance(t, int):
                pe.wait_ge(xT_lo, t - 1)
            for c in range(HC):
                ins = pe.transpose(PT[:, s, c * P:(c + 1) * P], xn[:, s, c * P:(c + 1) * P], ident[:])
            ins.then_inc(xn_t, 1)

        for s in range(2):
            turn_rows(s, s)
        with pe.Fori(1, NT // 2) as p:
            for s in range(2):
                turn_rows(p * 2 + s, s)

        def proj(out, stat, mov, chunks):
            n = [(c, s, m) for c in range(chunks) for s, m in PASSES]
            for j, (c, s, m) in enumerate(n):
                ins = pe.matmul(out, stat(s, c), mov(m, c), start=j == 0, stop=j == len(n) - 1)
            return ins

        def tokens(t):
            return lambda h, c: XT[h][:, c, t * GT:(t + 1) * GT]

        def weights(slot, half):
            return lambda h, c: WB[h][:, slot, half, c * P:(c + 1) * P]

        pe.wait_ge(xT_lo, NT)
        pe.wait_ge(w_lo, 2)

        def turn_logits(q):
            pe.wait_ge(logits_out, q + 1)
            if q >= 2:
                pe.wait_ge(logits_in, q - 1)
            for j in range(4):
                ins = pe.transpose(PT[:, q % 2, j * P:(j + 1) * P], logitsT[:, q % 2, j * P:(j + 1) * P], ident[:])
            ins.then_inc(logits_t, 1)

        for q in range(NG):
            if q >= 2:
                pe.wait_ge(logits_out, q - 1)
            ins = proj(PG[:, q % 2, :], weights(0, 0), tokens(q), HC).then_inc(router_mm, 1)
            if q >= 1:
                turn_logits(q - 1)
        turn_logits(NG - 1)

        def gate_up(n, slot, t):
            q = n * NG + t
            if not isinstance(q, int) or q >= 2:
                pe.wait_ge(silu_done, q - 1)
            proj(PG[:, t % 2, :], weights(slot, 0), tokens(t), HC).then_inc(gate_mm, 1)
            if not isinstance(q, int) or q >= 2:
                pe.wait_ge(prod_done, q - 1)
            proj(PU[:, t % 2, :], weights(slot, 1), tokens(t), HC).then_inc(up_mm, 1)

        for n in range(NS):
            pe.wait_ge(w_lo, 2 * (SHARED + n) + 2)
            for t in range(NG):
                gate_up(n, (SHARED + n) % 2, t)

        def down(chunks, weight, lo, mm, done, t, s):
            pe.wait_ge(lo, t + 1)
            if not isinstance(t, int) or t >= 2:
                pe.wait_ge(done, t - 1)
            return proj(PT[:, s, :], lambda h, c: DL[h][:, s, c, :], weight, chunks).then_inc(mm, 1)

        def down_w(h, c):
            return WD[h][:, c, :]

        pe.wait_ge(coeff_done, 1)
        for q in range(NG):
            if q >= 2:
                pe.wait_ge(coeff_out, q - 1)
            for j in range(4):
                ins = pe.transpose(PT[:, q % 2, j * P:(j + 1) * P], PR_[:, q * 4 + j, 0:E], ident[:])
            ins.then_inc(coeff_t, 1)
        pe.wait_ge(coeff_out, NG)
        pe.wait_ge(w_lo, 2 * SDOWN + 4)
        for s in range(2):
            down(4, down_w, sd_lo, sd_mm, sd_out, s, s)
        with pe.Fori(1, NT // 2) as p:
            for s in range(2):
                down(4, down_w, sd_lo, sd_mm, sd_out, p * 2 + s, s)
        def c_rows(k, t):
            if t == 0:
                pe.wait_ge(mr_ready, k + 1)
            if not isinstance(k, int) or k * NG + t >= 2:
                pe.wait_ge(cb_out, k * NG + t - 1)
            pe.matmul(PT[:, t % 2, :], MR[:], coeffT[:, t * GT:(t + 1) * GT], start=True, stop=True).then_inc(cb_mm, 1)

        pe.wait_ge(sd_out, NT)
        for t in range(NG):
            c_rows(0, t)

        def experts(k, last):
            for i in range(HALF):
                pe.wait_ge(w_lo, (k * HALF + EXPERT + i) * 2 + 2)
                for t in range(NG):
                    gate_up(k * HALF + NS + i, (EXPERT + i) % 2, t)
                    if i == HALF - 1 and not last:
                        c_rows(k + 1, t)
        with pe.Fori(0, KB - 1) as k:
            experts(k, False)
        experts(KB - 1, True)

        pe.wait_ge(w_lo, 2 * DOWN + 2)
        pe.wait_ge(cb_out, KB * NG)
        for s in range(2):
            down(2, down_w, d_lo, d_mm, d_out, s, s)
        with pe.Fori(1, NT // 2) as p:
            for s in range(2):
                down(2, down_w, d_lo, d_mm, d_out, p * 2 + s, s)


def build(nc, a, out):
    with ExitStack() as whole:
        X = whole.enter_context(nc.sbuf_tensor("x_rows", [P, NT, HID], F32))
        ident = whole.enter_context(nc.sbuf_tensor("ident", [P, P], F32))
        x1_mv = whole.enter_context(nc.sbuf_tensor("x1_mean_var", [P, NT, 2], F32))
        with ExitStack() as ctx:
            build_attention(nc, ctx, a, X, ident, x1_mv)
        with ExitStack() as ctx:
            build_ffn(nc, ctx, a, X, ident, x1_mv, out)


def constants():
    p = np.arange(P)
    key = (np.arange(4 * W) // (2 * W) - 1) * W + np.arange(4 * W) % W
    rel = key[None, :] - (p % W)[:, None]
    inside = (rel <= 0) & (rel > -W)
    slope = np.power(np.float32(2.0), np.float32(-8.0) * np.arange(H, dtype=np.float32) / np.float32(H))
    pair = np.arange(2 * HK)
    heads = (pair // 2 * G + pair % 2 * 2)[None, :] + (p // W)[:, None]
    return {
        "identity": np.eye(P, dtype=np.float32),
        "head_rows": (p[:, None] // D == np.arange(HK)[None, :]).astype(np.float32),
        "slopes": (slope[heads] * np.float32(D ** 0.5)).astype(np.float32),
        "rel_pen": np.stack([rel, np.where(inside, 0.0, MASKED)], 1).astype(np.float32),
    }


def kernel(**inputs):
    import concourse.bacc as bacc
    from concourse.bass_utils import run_bass_kernel_spmd

    nc = bacc.Bacc("TRN2", target_bir_lowering=False, num_devices=1)
    arrays, aps = {}, {}
    for name, v in {**inputs, **constants()}.items():
        v = np.ascontiguousarray(v)
        arrays[f"in_{name}"] = v
        aps[name] = nc.dram_tensor(f"in_{name}", v.shape, mybir.dt.from_np(v.dtype), kind="ExternalInput").ap()
    out = nc.dram_tensor("out", (B, T, HID), F32, kind="ExternalOutput").ap()
    build(nc, aps, out)
    return run_bass_kernel_spmd(nc, [arrays], core_ids=[0]).results[0]["out"]
```

```python
from contextlib import ExitStack

import numpy as np

import concourse.bass as bass
from concourse import mybir

ALU = mybir.AluOpType
ACT = mybir.ActivationFunctionType
AX = mybir.AxisListType
F32 = mybir.dt.float32
F32R = mybir.dt.float32r

P = 128
B, T, HID = 8, 256, 512
H, HK = 32, 8
G = H // HK
D = HID // H
W = 64
NB = T // W
HC = HID // P
TB = T // P
NT = B * TB
UNITS = HK * NB
RING = 4
LN_EPS = 1e-5
BANKS = 3
MASKED = -3.0e38
PASSES = (("hi", "hi"), ("lo", "hi"), ("hi", "lo"))
PARTS = len(PASSES)

E, TOPK, KB, FI = 128, 4, 8, 256
FS = 512
FFN_EPS = 1e-8
NG = 4
GT = B * T // NG


def wait_alone(eng, sem, value, passed):
    eng.wait_ge(sem, value)
    eng.sem_inc(passed, 1)


def newton_rsqrt(dve, done, count, var_eps, root, rstd, tmp):
    def link(ins):
        count[0] += 1
        ins.then_inc(done, 1)
        dve.wait_ge(done, count[0])
    link(dve.reciprocal(rstd, root))
    link(dve.tensor_tensor(tmp, rstd, rstd, ALU.mult))
    link(dve.tensor_tensor(tmp, tmp, var_eps, ALU.mult))
    link(dve.tensor_scalar(tmp, tmp, -0.5, 1.5, ALU.mult, ALU.add))
    link(dve.tensor_tensor(rstd, rstd, tmp, ALU.mult))


def build_attention(nc, ctx, a, X, ident, x1_mv):
    def sb(name, shape, dt=F32):
        return ctx.enter_context(nc.sbuf_tensor(name, shape, dt))

    def ps(name, shape):
        return ctx.enter_context(nc.psum_tensor(name, shape, F32))

    def sem(name):
        return ctx.enter_context(nc.semaphore(name))

    WQ = {h: sb(f"wq_{h}", [P, 2 * HC, HID], F32R) for h in ("hi", "lo")}
    WKV = {h: sb(f"wkv_{h}", [P, 4, HC, P], F32R) for h in ("hi", "lo")}
    WO = {h: sb(f"wo_{h}", [P, HC, HID], F32R) for h in ("hi", "lo")}
    AT = {h: sb(f"actT_{h}", [P, 2 * HC, T], F32R) for h in ("hi", "lo")}
    Q = {h: sb(f"qT_{h}", [P, 2, NB, 2, W], F32R) for h in ("hi", "lo")}
    K = {h: sb(f"kT_{h}", [P, NB, 2, W], F32R) for h in ("hi", "lo")}
    QS = sb("q_stack", [P, HK // 2, 2, NB, 2, W], F32R)
    KS = sb("k_stack", [P, HK // 2, NB * 2 * W], F32R)
    def rows_in(view):
        return view[:].rearrange("p a i r w -> p (a i r w)").rearrange("p (t d) -> p t d", t=TB).bitcast(F32)
    ctx_rows, xn = rows_in(Q["lo"]), rows_in(Q["hi"])
    VA = sb("v_ones", [P, NB, HK, 2 * D])
    bias = sb("bias", [P, HK * 2, 4 * W])
    SC = sb("scores_sb", [P, RING, 2, 4 * W])
    NM = sb("neg_max", [P, RING, 2])
    PT = sb("probsT", [P, 2, 2 * NB, G, W])
    OS = sb("oT_sums", [P, T])
    RI = sb("inv_sums", [P, TB, G])
    OT = {h: sb(f"oT_{h}", [P, TB, HC, P], F32R) for h in ("hi", "lo")}
    O = sb("o_rows", [P, TB, HID])
    VT = PT[:, 0, 0:2].rearrange("p h r q -> p (h r q)").rearrange("p (j s w) -> p j s w", j=NB, s=2)
    stage = PT[:, :, :, :, :].rearrange("p b h r q -> p (b h r q)").rearrange("p (s n) -> p s n", s=4)
    rel_pen = SC[:, 0, :, :]
    slopes = sb("slopes", [P, 2 * HK])
    stats = sb("stats", [P, NT, 6])
    x1_stats, batch_mv = sb("x1_stats", [P, TB, 6]), sb("batch_mean_var", [P, TB, 2])
    mv = sb("mean_var", [P, NT, 2])
    var_eps = sb("var_eps", [P, NT])
    root = sb("root", [P, NT])
    rstd = sb("rstd", [P, NT])
    tmp = sb("tmp", [P, NT])
    gate = sb("gate", [P, 1])
    tg = sb("tanh_gate", [P, 1])

    PJ = ps("ps_proj", [P, 2, HID])
    PS = ps("ps_scores", [P, BANKS, 2, 4 * W])
    PX = ps("ps_probsT", [P, 2, 2, 2, P])
    PON = ps("ps_o", [P, 2, T])
    PO, PN = PON[:, 0, :], PON[:, 1, :]

    consts_in, ident_in, x_in, ctx_in = sem("consts_in"), sem("ident_in"), [sem(f"x_in{n}") for n in range(B)], sem("ctx_in")
    stage_in = [sem(f"stage_in{n}") for n in range(8)]
    weights_hi, chain, root_done, tg_done = sem("weights_hi"), sem("chain"), sem("root_done"), sem("tg_done")
    weights_lo = [sem("weights_lo_pool"), sem("weights_lo_dve")]
    pool_ready, dve_passed = sem("pool_ready"), sem("dve_passed")
    xn_ready, prep_t, prep_hi, prep_lo = sem("xn_ready"), sem("prep_t"), sem("prep_hi"), sem("prep_lo")
    proj_mm, proj_hi, proj_lo = sem("proj_mm"), sem("proj_hi"), sem("proj_lo")
    v_turned, v_ready = sem("v_turned"), sem("v_ready")
    stacked, dma_passed = sem("stacked"), sem("dma_passed")
    k_third_in = [sem(f"k_third_in{g}") for g in range(HK)]
    q_third_in = [sem(f"q_third_in{g}") for g in range(HK)]
    k_in, q_in = [sem(f"k_in{g}") for g in range(HK)], [sem(f"q_in{g}") for g in range(HK)]
    scores_mm, sc_done, exp_done, probs_t = sem("scores_mm"), sem("sc_done"), sem("exp_done"), sem("probs_t")
    pt_done = [sem("pt_done_act"), sem("pt_done_dve")]
    pv_mm, oT_out, o_turned, inv_done, o_done = (
        sem("pv_mm"), sem("oT_out"), sem("o_turned"), sem("inv_done"), sem("o_done"))
    oT_mm, oT_hi, oT_lo, wo_mm, x1_done, ve_done, x1_st, x1_ag = (
        sem("oT_mm"), sem("oT_hi"), sem("oT_lo"), sem("wo_mm"), sem("x1_done"), sem("ve_done"), sem("x1_st"),
        sem("x1_ag"))

    x_t = a["x"].rearrange("b (t p) d -> p b t d", p=P)
    ctx_t = a["ctx_2048"].rearrange("b (t p) d -> p b t d", p=P)

    wq_d = a["L0_xattn_Wq"].rearrange("(c p) n -> p c n", p=P)
    wo_d = a["L0_xattn_Wo"].rearrange("(c p) n -> p c n", p=P)
    kv_d = [a[f"L0_xattn_{n}"].rearrange("(c p) n -> p c n", p=P) for n in ("Wsk", "Wk", "Wsv", "Wv")]

    def q_order(part, c):
        return part[:, c, :].rearrange("p (r g d) -> p g r d", r=G, g=HK)

    def kv_half(m):
        return kv_d[m], {h: WKV[h][:, m] for h in WKV}, ("c n", dict(c=HC))

    halves = [kv_half(0), kv_half(1)]
    for c in range(2 * HC):
        halves.append((wq_d[:, c, :], {h: q_order(WQ[h], c) for h in WQ}, ("g r d", dict(g=HK, r=G))))
    halves += [kv_half(2), kv_half(3)]
    for c in range(HC):
        halves.append((wo_d[:, c, :], {h: WO[h][:, c, :] for h in WO}, None))
    FIRST_Q, FIRST_V, FIRST_O = 2, 2 + 2 * HC, 4 + 2 * HC

    def raw(n):
        v = stage[:, (n // 2) % 4, (n % 2) * HID:(n % 2 + 1) * HID]
        shape = halves[n][2]
        return v.rearrange(f"p ({shape[0]}) -> p {shape[0]}", **shape[1]) if shape else v

    def probs_out(eng, nce, b, u):
        g, i = divmod(u, NB)
        if i < 2 and g >= 2:
            eng.wait_ge(pv_mm, b * HK + g - 1)
        if u < 2:
            eng.wait_ge(v_turned, b + 1)
        eng.wait_ge(probs_t, b * UNITS + u + 1)
        first = 1 if i == 0 else 0
        dst = PT[:, g % 2, 2 * i + first:2 * i + 2].rearrange("p h r q -> p (h r q)")
        src = PX[:, u % 2, first:2].rearrange("p h k q -> p (h k q)")
        if u % 2 == 0:
            nce.activation(dst, src, ACT.Copy).then_inc(pt_done[0], 1)
        else:
            nce.tensor_copy(dst, src).then_inc(pt_done[1], 1)

    def wait_split(eng, n):
        eng.wait_ge(weights_lo[n % 2], n // 2 + 1)

    def split_lo(eng, n):
        eng.wait_ge(weights_hi, n + 1)
        eng.tensor_tensor(halves[n][1]["lo"], raw(n), halves[n][1]["hi"].bitcast(F32),
                          ALU.subtract).then_inc(weights_lo[n % 2], 1)

    def stack_k(eng, g, j):
        rows = K[PASSES[j][1]][g * D:(g + 1) * D].rearrange("p j s w -> p (j s w)")
        return eng.dma_start(KS[stack_rows(g, j), g // 2, :].bitcast(F32), rows.bitcast(F32))

    def stack_q(eng, g, j):
        rows = Q[PASSES[j][0]][g * D:(g + 1) * D].rearrange("p a i r w -> p (a i r w)")
        return eng.dma_start(QS[stack_rows(g, j), g // 2].rearrange("p a i r w -> p (a i r w)").bitcast(F32),
                             rows.bitcast(F32))

    def stack_rows(g, j=None):
        first = 64 * (g % 2)
        return slice(first, first + PARTS * D) if j is None else slice(first + j * D, first + (j + 1) * D)

    def tile_columns(i):
        src, t = i // TB, i % TB
        return slice(None), slice(src * HC, (src + 1) * HC), slice(t * P, (t + 1) * P)

    def row(view, n):
        return view[:, bass.ds(n, 1), :].rearrange("p o d -> p (o d)")

    LN_GROUPS = [(0, TB), (TB, 2 * TB), (2 * TB, NT)]

    TURN, OUT = 2, 3
    PV, PV_OUT, TURN_O, NORM = 7, 8, 9, 10
    TURN_V = 0
    LAST_TURN_O, TURN_ROWS, TIMES_WO = 0, 2, [5, 6]
    PREP = [9, 11, 13, 15]
    JOBS = [18, 20, 22, 24, 26]
    EARLY = HK - 1
    STACKS = ([("k", g) for g in range(EARLY)] + [("q", g) for g in range(EARLY)] +
              [(what, g) for g in range(EARLY, HK) for what in "kq"])

    block = ctx.enter_context(nc.Block())

    @block.sync
    def _(sp):
        sp.dma_start(ctx_rows, ctx_t[:, 0]).then_inc(ctx_in, 16)
        sp.dma_start(ident[:], a["identity"]).then_inc(ident_in, 16)
        sp.dma_start(X[:, 0:TB, :], x_t[:, 0]).then_inc(x_in[0], 16)
        for n in range(len(halves)):
            if n >= 8:
                wait_split(sp, n - 8)
            src = halves[n][0]
            dst = stage[:, (n // 2) % 4, (n % 2) * HID:(n % 2 + 1) * HID]
            if len(src.shape) == 3:
                dst = dst.rearrange("p (c n) -> p c n", c=HC)
            sp.dma_start(dst, src).then_inc(stage_in[n % 8], 16)
            if n == 7:
                for dst, src in ((slopes[:], a["slopes"]), (rel_pen, a["rel_pen"]),
                                 (gate[:], a["g_xattn"].partition_broadcast(P))):
                    sp.dma_start(dst, src).then_inc(consts_in, 16)
        for n in range(1, B):
            sp.dma_start(X[:, TB * n:TB * (n + 1), :], x_t[:, n]).then_inc(x_in[n], 16)

        def stack(b, first=False):
            for what, g in STACKS:
                if what == "k":
                    if not first:
                        sp.wait_ge(scores_mm, b * UNITS - UNITS + NB * (g + 1))
                    sp.wait_ge(proj_lo, b * 5 + 1)
                    for j in range(2):
                        stack_k(sp, g, j).then_inc(k_in[g], 16)
                else:
                    sp.wait_ge(proj_lo, b * 5 + 5)
                    for j in range(2):
                        stack_q(sp, g, j).then_inc(q_in[g], 16)
            for g in range(HK):
                sp.wait_ge(k_in[g], b * 32 + 32)
                sp.wait_ge(k_third_in[g], b * 16 + 16)
                sp.wait_ge(q_in[g], b * 32 + 32)
                sp.wait_ge(q_third_in[g], b * 16 + 16)
            sp.sem_inc(stacked, 1)

        def next_ctx(b):
            sp.wait_ge(v_turned, b)
            sp.dma_start(ctx_rows, ctx_t[:, bass.ds(b, 1)].rearrange("p b t d -> p (b t) d")).then_inc(ctx_in, 16)

        stack(0, True)
        next_ctx(1)
        with sp.Fori(1, B - 1) as b:
            stack(b)
            next_ctx(b + 1)
        stack(B - 1)

    @block.gpsimd
    def _(pool):
        def stack(b, first=False):
            for what, g in STACKS:
                if what == "k":
                    if not first:
                        wait_alone(pool, scores_mm, b * UNITS - UNITS + NB * (g + 1), dma_passed)
                    wait_alone(pool, proj_lo, b * 5 + 1, dma_passed)
                    stack_k(pool, g, 2).then_inc(k_third_in[g], 16)
                else:
                    wait_alone(pool, proj_lo, b * 5 + 5, dma_passed)
                    stack_q(pool, g, 2).then_inc(q_third_in[g], 16)

        pool.memset(VA[:], 1.0).then_inc(pool_ready, 1)
        for n in range(0, FIRST_O, 2):
            split_lo(pool, n)
        stack(0, True)
        for n in range(FIRST_O, len(halves), 2):
            split_lo(pool, n)
        with pool.Fori(1, B) as b:
            stack(b)

    @block.scalar
    def _(act):
        def split_hi(n):
            act.wait_ge(stage_in[n % 8], 16 * (n // 8) + 16)
            act.activation(halves[n][1]["hi"], raw(n), ACT.Copy).then_inc(weights_hi, 1)

        def prep(b, i):
            act.wait_ge(prep_t, b * 4 + i + 1)
            act.activation(AT["hi"][tile_columns(i)], PJ[:, i % 2, :].rearrange("p (c n) -> p c n", c=HC),
                           ACT.Copy).then_inc(prep_hi, 1)

        def proj_out(b, n, first):
            act.wait_ge(proj_mm, b * 6 + n + 1)
            if n == 0 and not first:
                act.wait_ge(stacked, b)
            if 1 <= n <= G:
                r = n - 1
                act.activation(Q["hi"][:, r // 2, :, r % 2, :],
                               PJ[:, n % 2, 0:T].rearrange("p (i w) -> p i w", i=NB), ACT.Copy).then_inc(proj_hi, 1)
            else:
                dst = K["hi"][:] if n == 0 else VT
                act.activation(dst.rearrange("p j s w -> p s j w"),
                               PJ[:, n % 2, :].rearrange("p (s j w) -> p s j w", s=2, j=NB),
                               ACT.Copy).then_inc(proj_hi, 1)

        def exps(b, s):
            n = 2 * W if s % NB == 0 else 4 * W
            for pp in range(2):
                act.wait_ge(sc_done, b * 2 * UNITS + 2 * s + pp + 1)
                act.activation(SC[:, s % RING, pp, 0:n], SC[:, s % RING, pp, 0:n], ACT.Exp,
                               bias=NM[:, s % RING, pp:pp + 1], scale=-1.0).then_inc(exp_done, 1)

        def pv_out(b, g):
            act.wait_ge(pv_mm, b * HK + g + 1)
            if g >= 1:
                act.wait_ge(o_turned, b * HK + g)
            act.activation(OS[:], PO, ACT.Copy).then_inc(oT_out, 1)

        def oT_high(b, t):
            act.wait_ge(oT_mm, b * TB + t + 1)
            act.activation(OT["hi"][:, t], PJ[:, t, :].rearrange("p (c n) -> p c n", c=HC), ACT.Copy).then_inc(oT_hi, 1)

        def boundary(b, before, after):
            jobs = list(range(len(JOBS) if before else 0, 5)) if after else []
            if before:
                pv_out(b - 1, HK - 2)
            for n in jobs[:1]:
                proj_out(b, n, not before)
            if before:
                probs_out(act, nc.scalar, b - 1, UNITS - 2)
            for n in jobs[1:]:
                proj_out(b, n, not before)
            if before:
                pv_out(b - 1, HK - 1)
            if after:
                proj_out(b, 5, not before)
            if before and not after:
                for t in range(TB):
                    oT_high(b - 1, t)

        def units(b, first, last):
            for s in range(UNITS):
                if s >= OUT and (s - OUT) % 2 == 0:
                    probs_out(act, nc.scalar, b, s - OUT)
                g, r = divmod(s - PV_OUT, NB)
                if r == 0 and g >= 0:
                    pv_out(b, g)
                exps(b, s)
                if not first and s == TURN_ROWS:
                    for t in range(TB):
                        oT_high(b - 1, t)
                if first and s == 25:
                    roots(2)
                if not last and s - 1 in PREP:
                    prep(b + 1, PREP.index(s - 1))
                if not last and s - 1 in JOBS:
                    proj_out(b + 1, JOBS.index(s - 1), False)

        def roots(n):
            act.wait_ge(ve_done, n + 1)
            ts = slice(*LN_GROUPS[n])
            act.activation(root[:, ts], var_eps[:, ts], ACT.Sqrt).then_inc(root_done, 1)

        roots(0)
        prep(0, 0)
        prep(0, 1)
        for n in range(4):
            split_hi(n)
        prep(0, 2)
        prep(0, 3)
        for n in range(4, 12):
            split_hi(n)
        boundary(0, False, True)
        for n in range(12, len(halves)):
            split_hi(n)
        roots(1)
        act.wait_ge(consts_in, 48)
        act.activation(tg[:], gate[:], ACT.Tanh).then_inc(tg_done, 1)
        for n in range(len(halves) - 2, len(halves)):
            wait_split(act, n)
        units(0, True, False)
        with act.Fori(1, B - 1) as b:
            boundary(b, True, True)
            units(b, False, False)
        boundary(B - 1, True, True)
        units(B - 1, False, True)
        boundary(B, True, False)

    @block.vector
    def _(dve):
        count = [0]

        def link(ins):
            count[0] += 1
            ins.then_inc(chain, 1)
            dve.wait_ge(chain, count[0])

        def one_row_stats(t):
            dve.wait_ge(x_in[t // TB], 16)
            link(dve.bn_stats(stats[:, t, :], X[:, t, :]))
            link(dve.bn_aggr(mv[:, t, :], stats[:, t, :]))

        def variances(first, last):
            ts = slice(first, last)
            dve.tensor_scalar(var_eps[:, ts], mv[:, ts, 1], LN_EPS, None, ALU.add).then_inc(ve_done, 1)

        def inverse_roots(first, last):
            dve.wait_ge(root_done, LN_GROUPS.index((first, last)) + 1)
            ts = slice(first, last)
            newton_rsqrt(dve, chain, count, var_eps[:, ts], root[:, ts], rstd[:, ts], tmp[:, ts])

        def normalise(b, t, first=False):
            if t == 0 and not first:
                wait_alone(dve, stacked, b, dve_passed)
            one = bass.ds(b * TB + t, 1)
            dve.tensor_scalar(xn[:, t, :], row(X, b * TB + t), mv[:, one, 0], rstd[:, one],
                              ALU.subtract, ALU.mult).then_inc(xn_ready, 1)

        def prep(b, i):
            dve.wait_ge(prep_hi, b * 4 + i + 1)
            dve.tensor_tensor(AT["lo"][tile_columns(i)], PJ[:, i % 2, :].rearrange("p (c n) -> p c n", c=HC),
                              AT["hi"][tile_columns(i)].bitcast(F32), ALU.subtract).then_inc(prep_lo, 1)

        def proj_out(b, n):
            dve.wait_ge(proj_hi, b * 6 + n + 1)
            if 1 <= n <= G:
                r = n - 1
                dve.tensor_tensor(Q["lo"][:, r // 2, :, r % 2, :],
                                  PJ[:, n % 2, 0:T].rearrange("p (i w) -> p i w", i=NB),
                                  Q["hi"][:, r // 2, :, r % 2, :].bitcast(F32), ALU.subtract).then_inc(proj_lo, 1)
            else:
                dve.tensor_tensor(K["lo"][:].rearrange("p j s w -> p s j w"),
                                  PJ[:, n % 2, :].rearrange("p (s j w) -> p s j w", s=2, j=NB),
                                  K["hi"][:].bitcast(F32).rearrange("p j s w -> p s j w"),
                                  ALU.subtract).then_inc(proj_lo, 1)

        def maxima(b, s):
            g, i = divmod(s, NB)
            n = 2 * W if i == 0 else 4 * W
            if s >= RING:
                dve.wait_ge(probs_t, b * UNITS + s - RING + 1)
            wait_alone(dve, scores_mm, b * UNITS + s + 1, dve_passed)
            for pp in range(2):
                dve.tensor_tensor_reduce(SC[:, s % RING, pp, 0:n], PS[:, s % BANKS, pp, 0:n],
                                         bias[:, 2 * g + pp, 4 * W - n:4 * W], -float(D) ** -0.5, 3e38,
                                         ALU.add, ALU.min, NM[:, s % RING, pp:pp + 1]).then_inc(sc_done, 1)

        def norm(b, g):
            dve.wait_ge(o_turned, b * HK + g + 1)
            v = PN.rearrange("p (t r e) -> p t r e", t=TB, r=G)
            dve.reciprocal(RI[:], v[:, :, :, D]).then_inc(inv_done, 1)
            dve.wait_ge(inv_done, b * HK + g + 1)
            dve.tensor_tensor(O[:, :, g * G * D:(g + 1) * G * D].rearrange("p t (r d) -> p t r d", r=G),
                              v[:, :, :, 0:D], RI[:].unsqueeze(3).broadcast_to([P, TB, G, D]),
                              ALU.mult).then_inc(o_done, 1)

        def oT_low(b, t):
            dve.wait_ge(oT_hi, b * TB + t + 1)
            dve.tensor_tensor(OT["lo"][:, t], PJ[:, t, :].rearrange("p (c n) -> p c n", c=HC),
                              OT["hi"][:, t].bitcast(F32), ALU.subtract).then_inc(oT_lo, 1)

        def residual(b, t):
            x1 = row(X, b * TB + t)
            dve.wait_ge(wo_mm, b * TB + t + 1)
            dve.scalar_tensor_tensor(out=x1, in0=PJ[:, t, :], scalar=tg[:, 0:1],
                                     in1=x1, op0=ALU.mult, op1=ALU.add).then_inc(x1_done, 1)
            wait_alone(dve, x1_done, b * TB + t + 1, dve_passed)
            dve.bn_stats(x1_stats[:, t, :], x1).then_inc(x1_st, 1)
            wait_alone(dve, x1_st, b * TB + t + 1, dve_passed)
            dve.bn_aggr(batch_mv[:, t, :], x1_stats[:, t, :]).then_inc(x1_ag, 1)
            dve.wait_ge(x1_ag, b * TB + t + 1)
            dve.tensor_copy(row(x1_mv, b * TB + t), batch_mv[:, t, :])

        def boundary(b, before, after):
            jobs = list(range(len(JOBS) if before else 0, 5)) if after else []
            if before:
                probs_out(dve, nc.vector, b - 1, UNITS - 3)
            for n in jobs[:1]:
                proj_out(b, n)
            if before:
                norm(b - 1, HK - 2)
                probs_out(dve, nc.vector, b - 1, UNITS - 1)
            for n in jobs[1:]:
                proj_out(b, n)
            if before and not after:
                norm(b - 1, HK - 1)
                for t in range(TB):
                    oT_low(b - 1, t)
                for t in range(TB):
                    residual(b - 1, t)

        def units(b, first, last):
            for s in range(UNITS):
                if s >= OUT and (s - OUT) % 2 == 1:
                    probs_out(dve, nc.vector, b, s - OUT)
                g, r = divmod(s - NORM, NB)
                if r == 0 and g >= 0:
                    norm(b, g)
                if s == TURN_V + 1:
                    dve.wait_ge(v_turned, b + 1)
                    dve.tensor_copy(VA[:, :, :, 0:D], PJ[:, 0, :].rearrange("p (j g d) -> p j g d", j=NB, g=HK)
                                    ).then_inc(v_ready, 1)
                if not first:
                    if s == LAST_TURN_O + 1:
                        norm(b - 1, HK - 1)
                    for t in range(TB):
                        if s == TURN_ROWS + 2:
                            oT_low(b - 1, t)
                        if s == TIMES_WO[t] + 2:
                            residual(b - 1, t)
                maxima(b, s)
                if first and 12 <= s < 12 + NT - 2 * TB:
                    one_row_stats(s - 12 + 2 * TB)
                if first and s == 24:
                    variances(*LN_GROUPS[2])
                if first and s == 27:
                    inverse_roots(*LN_GROUPS[2])
                if not last:
                    if 8 <= s < 8 + TB:
                        normalise(b + 1, s - 8)
                    if s - 2 in PREP:
                        prep(b + 1, PREP.index(s - 2))
                    if s - 2 in JOBS:
                        proj_out(b + 1, JOBS.index(s - 2))

        for t in range(TB):
            one_row_stats(t)
        variances(*LN_GROUPS[0])
        inverse_roots(*LN_GROUPS[0])
        for t in range(TB):
            normalise(0, t, True)
        prep(0, 0)
        prep(0, 1)
        split_lo(dve, 1)
        split_lo(dve, 3)
        prep(0, 2)
        prep(0, 3)
        for n in range(5, 12, 2):
            split_lo(dve, n)
        dve.wait_ge(consts_in, 48)
        for k in range(2 * HK):
            ins = dve.scalar_tensor_tensor(out=bias[:, k, :], in0=rel_pen[:, 0, :], scalar=slopes[:, k:k + 1],
                                           in1=rel_pen[:, 1, :], op0=ALU.mult, op1=ALU.add)
        link(ins)
        boundary(0, False, True)
        for n in range(13, len(halves), 2):
            split_lo(dve, n)
        for t in range(TB, 2 * TB):
            one_row_stats(t)
        variances(*LN_GROUPS[1])
        inverse_roots(*LN_GROUPS[1])
        dve.wait_ge(pool_ready, 1)
        dve.wait_ge(tg_done, 1)
        for n in range(len(halves) - 2, len(halves)):
            wait_split(dve, n)
        units(0, True, False)
        with dve.Fori(1, B - 1) as b:
            boundary(b, True, True)
            units(b, False, False)
        boundary(B - 1, True, True)
        units(B - 1, False, True)
        boundary(B, True, False)

    @block.tensor
    def _(pe):
        def product(out, stat, mov, chunks, before=None):
            for c in chunks:
                if before:
                    before(c)
                for j, (s, m) in enumerate(PASSES):
                    ins = pe.matmul(out, stat(s, c), mov(m, c), start=c == chunks[0] and j == 0,
                                    stop=c == chunks[-1] and j == 2)
            return ins

        def prep(b, i):
            src, t = i // TB, i % TB
            if src == 0:
                pe.wait_ge(ctx_in, b * 16 + 16)
            else:
                pe.wait_ge(xn_ready, b * TB + t + 1)
            if i >= 2:
                pe.wait_ge(prep_lo, b * 4 + i - 1)
            rows = ctx_rows if src == 0 else xn
            for c in range(HC):
                ins = pe.transpose(PJ[:, i % 2, c * P:(c + 1) * P], rows[:, t, c * P:(c + 1) * P], ident[:])
            ins.then_inc(prep_t, 1)

        def proj(b, n, first):
            if n == 0:
                pe.wait_ge(prep_lo, b * 4 + 4)
            if n >= 2:
                pe.wait_ge(proj_lo, b * 5 + n - 1)
            if 1 <= n <= G:
                ins = product(PJ[:, n % 2, 0:T], lambda h, c: WQ[h][:, c, (n - 1) * P:n * P],
                              lambda h, c: AT[h][:, c, :], range(2 * HC),
                              (lambda c: wait_split(pe, FIRST_Q + c)) if first and n == 1 else None)
            else:
                m = 0 if n == 0 else 2
                for src in range(2):
                    if first:
                        wait_split(pe, (0 if n == 0 else FIRST_V) + src)
                    ins = product(PJ[:, n % 2, src * T:(src + 1) * T], lambda h, c: WKV[h][:, m + src, c, :],
                                  lambda h, c: AT[h][:, src * HC + c, :], range(HC))
            ins.then_inc(proj_mm, 1)

        def turn_v(b):
            pe.wait_ge(proj_hi, b * 6 + 6)
            pe.wait_ge(proj_lo, b * 5 + 5)
            for j in range(NB):
                ins = pe.transpose(PJ[:, 0, j * P:(j + 1) * P], VT[:, j].rearrange("p s w -> p (s w)"), ident[:])
            ins.then_inc(v_turned, 1)

        def score(b, s, first):
            g, i = divmod(s, NB)
            first_col = max(i - 1, 0) * 2 * W
            if i == 0:
                pe.wait_ge(k_in[g], b * 32 + 32)
                pe.wait_ge(k_third_in[g], b * 16 + 16)
                pe.wait_ge(q_in[g], b * 32 + 32)
                pe.wait_ge(q_third_in[g], b * 16 + 16)
            if s >= BANKS:
                pe.wait_ge(sc_done, b * 2 * UNITS + 2 * (s - BANKS + 1))
            for pp in range(2):
                ins = pe.matmul(PS[:, s % BANKS, pp, :], QS[stack_rows(g), g // 2, pp, i].rearrange("p r w -> p (r w)"),
                                KS[stack_rows(g), g // 2, first_col:first_col + 4 * W], start=True, stop=True)
            ins.then_inc(scores_mm, 1)

        def turn_probs(b, u):
            g, i = divmod(u, NB)
            pe.wait_ge(exp_done, b * 2 * UNITS + 2 * u + 2)
            if u >= 2:
                pe.wait_ge(pt_done[u % 2], b * UNITS // 2 + u // 2)
            first = 1 if i == 0 else 0
            for h in range(first, 2):
                for pp in range(2):
                    ins = pe.transpose(PX[:, u % 2, h, pp, :], SC[:, u % RING, pp, (h - first) * P:(h - first + 1) * P],
                                       ident[:])
            ins.then_inc(probs_t, 1)

        def times_v(b, g):
            if g == 0:
                pe.wait_ge(v_ready, b + 1)
            for e in range(2):
                pe.wait_ge(pt_done[e], b * UNITS // 2 + 2 * (g + 1))
            if g >= 1:
                pe.wait_ge(o_done, b * HK + g)
            for j in range(NB):
                n = min(2 * W, T - j * W)
                for r in range(G):
                    ins = pe.matmul(PO[32 * r:32 * r + 2 * D, j * W:j * W + n], VA[:, j, g, :],
                                    PT[:, g % 2, 2 * j + 1:2 * j + 1 + n // W, r, :],
                                    start=j == 0, stop=j == NB - 1, skip_group_check=True)
            ins.then_inc(pv_mm, 1)

        def turn_o(b, g):
            pe.wait_ge(oT_out, b * HK + g + 1)
            for t in range(TB):
                ins = pe.transpose(PN[:, t * P:(t + 1) * P], OS[:, t * P:(t + 1) * P], ident[:])
            ins.then_inc(o_turned, 1)

        def turn_rows(b):
            pe.wait_ge(o_done, b * HK + HK)
            for t in range(TB):
                for c in range(HC):
                    ins = pe.transpose(PJ[:, t, c * P:(c + 1) * P], O[:, t, c * P:(c + 1) * P], ident[:])
                ins.then_inc(oT_mm, 1)

        def times_wo(b, t):
            pe.wait_ge(oT_lo, b * TB + t + 1)
            product(PJ[:, t, :], lambda h, c: OT[h][:, t, c, :],
                    lambda h, c: WO[h][:, c, :], range(HC)).then_inc(wo_mm, 1)

        def boundary(b, before, after):
            first = not before
            jobs = list(range(len(JOBS) if before else 0, 5)) if after else []
            for n in jobs[:1]:
                proj(b, n, first)
            if before:
                turn_probs(b - 1, UNITS - 2)
                turn_o(b - 1, HK - 2)
                turn_probs(b - 1, UNITS - 1)
            for n in jobs[1:]:
                proj(b, n, first)
            if after:
                proj(b, 5, first)
            if before:
                times_v(b - 1, HK - 1)
            if before and not after:
                turn_o(b - 1, HK - 1)
                turn_rows(b - 1)
                for t in range(TB):
                    times_wo(b - 1, t)

        def units(b, first, last):
            for s in range(UNITS):
                score(b, s, first)
                if s >= TURN:
                    turn_probs(b, s - TURN)
                g, r = divmod(s - PV, NB)
                if r == 0 and g >= 0:
                    times_v(b, g)
                g, r = divmod(s - TURN_O, NB)
                if r == 0 and g >= 0:
                    turn_o(b, g)
                if s == TURN_V:
                    turn_v(b)
                if not first and s == LAST_TURN_O:
                    turn_o(b - 1, HK - 1)
                if not first and s == TURN_ROWS:
                    pe.wait_ge(v_ready, b + 1)
                    turn_rows(b - 1)
                for t in range(TB):
                    if not first and s == TIMES_WO[t]:
                        times_wo(b - 1, t)
                if not last and s in PREP:
                    if s == PREP[0]:
                        pe.wait_ge(v_ready, b + 1)
                        if not first:
                            pe.wait_ge(x1_done, b * TB)
                    prep(b + 1, PREP.index(s))
                if not last and s in JOBS:
                    proj(b + 1, JOBS.index(s), False)

        pe.wait_ge(ident_in, 16)
        for i in range(4):
            prep(0, i)
        boundary(0, False, True)
        units(0, True, False)
        for n in range(FIRST_O, len(halves)):
            wait_split(pe, n)
        with pe.Fori(1, B - 1) as b:
            boundary(b, True, True)
            units(b, False, False)
        boundary(B - 1, True, True)
        units(B - 1, False, True)
        boundary(B, True, False)


def build_ffn(nc, ctx, a, X, ident, x1_mv, out):
    def sb(name, shape, dt=F32):
        return ctx.enter_context(nc.sbuf_tensor(name, shape, dt))

    def ps(name, shape):
        return ctx.enter_context(nc.psum_tensor(name, shape, F32))

    def sem(name):
        return ctx.enter_context(nc.semaphore(name))

    TOK = B * T
    XT = {h: sb(f"xnT_{h}", [P, HC, TOK], F32R) for h in ("hi", "lo")}
    big = sb("big", [P, 4, TOK])
    hT = big[:, :, :]
    mixed, cB = big[:, 0:2, :], big[:, 2, :]
    WB = {h: sb(f"w_{h}", [P, 2, 2, 4 * P], F32R) for h in ("hi", "lo")}
    WD = {h: sb(f"w_down_{h}", [P, 4, HID], F32R) for h in ("hi", "lo")}
    raw = sb("w_raw", [P, 2, 2, 4 * P])
    DL = {h: sb(f"down_{h}", [P, 2, 4, P], F32R) for h in ("hi", "lo")}
    PR_ = sb("probs", [P, NT, E + 4])
    left = sb("probs_left", [P, NT * (E + 4)])
    probs_left = left[:, :].rearrange("p (t e) -> p t e", t=NT)
    coeffT = left[:, 0:TOK]
    SG = sb("silu_gate", [P, 2, GT])
    BS = sb("basis", [P, 2, GT])
    xn, logitsT = BS, SG
    MR = sb("mix_column", [P, P])
    amp = sb("amp", [P, KB, 2])
    amp2 = sb("amp2", [P, KB])
    mix = sb("mix", [P, KB])
    escale = sb("escale", [P, 1])
    col = {n: sb(n, [P, 1]) for n in ("mix_sum", "gate_f", "tanh_gate_f")}
    mv = x1_mv
    ln = {n: sb(n, [P, NT]) for n in ("var_eps1", "root1", "rstd1", "tmp1")}
    top8 = sb("top8", [P, NT, 8])
    per_tile = {n: sb(n, [P, NT]) for n in ("row_max", "row_sum", "row_inv", "top_sum", "top_inv")}

    PT = ps("ps_turn", [P, 2, GT])
    PG = ps("ps_gate", [P, 2, GT])
    PU = ps("ps_up", [P, 2, GT])

    consts_in, chain, root_done, tg_done = sem("f_consts"), sem("f_chain"), sem("f_root"), sem("f_tg")
    ve_done, ready = sem("f_var"), sem("f_ready")
    raw_in = [sem("raw_in0"), sem("raw_in1")]
    w_hi, w_lo = sem("w_hi_done"), sem("w_lo_done")
    xn_ready, xn_t, xT_hi, xT_lo = sem("f_xn"), sem("f_xnT"), sem("f_xT_hi"), sem("f_xT_lo")
    router_mm, logits_out, logits_t, logits_in = sem("router_mm"), sem("logits_out"), sem("logits_t"), sem("logits_in")
    shifted, exp_done, coeff_done, coeff_t, coeff_out = (
        sem("shifted"), sem("f_exp"), sem("coeff_done"), sem("coeff_t"), sem("coeff_out"))
    gate_mm, up_mm, silu_done, prod_done, basis_done, acc_done = (
        sem("gate_mm"), sem("up_mm"), sem("silu_done"), sem("prod_done"), sem("basis_done"), sem("acc_done"))
    mr_ready, cb_mm, cb_out = sem("mr_ready"), sem("cb_mm"), sem("cb_out")
    sd_hi, sd_lo, sd_mm, sd_out = sem("sd_hi"), sem("sd_lo"), sem("sd_mm"), sem("sd_out")
    d_hi, d_lo, d_mm, d_out, stored = sem("d_hi"), sem("d_lo"), sem("d_mm"), sem("d_out"), sem("stored")

    NS, NE = FS // P, KB * FI // P
    SHARED, SDOWN, EXPERT = 1, 1 + NS, 3 + NS
    DOWN = EXPERT + NE
    HALF = FI // P

    def cols(w, n):
        return w.rearrange("(c p) n -> p c n", p=P)[:, :, bass.ds(n * P, P)]

    block = ctx.enter_context(nc.Block())

    @block.sync
    def _(sp):
        for dst, src in ((amp[:], a["L0_ffn_amplitudes"]), (escale[:], a["L0_ffn_expert_scale"].rearrange("(e o) -> e o", o=1)),
                         (col["gate_f"][:], a["g_ffn"].partition_broadcast(P))):
            sp.dma_start(dst, src).then_inc(consts_in, 16)

        def load(idx, slot, first, second):
            if not isinstance(idx, int) or idx >= 2:
                sp.wait_ge(w_lo, (idx - 1) * 2)
            sp.dma_start(raw[:, slot, 0, :].rearrange("p (c n) -> p c n", c=first.shape[1])
                         if first.shape[1] * first.shape[2] == 4 * P else
                         raw[:, slot, 0, 0:2 * P].rearrange("p (c n) -> p c n", c=2), first).then_inc(raw_in[slot], 16)
            sp.dma_start(raw[:, slot, 1, :].rearrange("p (c n) -> p c n", c=second.shape[1])
                         if second.shape[1] * second.shape[2] == 4 * P else
                         raw[:, slot, 0, 2 * P:4 * P].rearrange("p (c n) -> p c n", c=2), second).then_inc(raw_in[slot], 16)

        router = cols(a["L0_ffn_w_router"], 0)
        load(0, 0, router[:, 0:2], router[:, 2:4])
        for n in range(NS):
            load(SHARED + n, (SHARED + n) % 2, cols(a["L0_ffn_shared_w_gate"], n), cols(a["L0_ffn_shared_w_up"], n))
        sdown = a["L0_ffn_shared_w_down"].rearrange("(c p) n -> p c n", p=P)
        for n in range(2):
            load(SDOWN + n, (SDOWN + n) % 2, sdown[:, 2 * n:2 * n + 1], sdown[:, 2 * n + 1:2 * n + 2])
        with sp.Fori(0, KB) as k:
            for i in range(HALF):
                load(k * HALF + EXPERT + i, (EXPERT + i) % 2, cols(a["L0_ffn_w_gate"], k * HALF + i),
                     cols(a["L0_ffn_w_up"], k * HALF + i))
        down = a["L0_ffn_w_down"].rearrange("(c p) n -> p c n", p=P)
        load(DOWN, DOWN % 2, down[:, 0:1], down[:, 1:2])
        out_t = out.rearrange("b (t p) d -> p (b t) d", p=P)
        with sp.Fori(0, NT) as t:
            sp.wait_ge(d_out, t + 1)
            sp.dma_start(out_t[:, bass.ds(t, 1)], X[:, bass.ds(t, 1), :]).then_inc(stored, 16)
        sp.wait_ge(stored, 16 * NT)

    def place(part, idx, slot):
        if isinstance(idx, int) and (SDOWN <= idx < EXPERT or idx == DOWN):
            c = 2 * (idx - SDOWN) if idx < DOWN else 0
            return WD[part][:, c:c + 2, :]
        return WB[part][:, slot]

    def at_tile(view, t):
        return view[:, :, bass.ds(t * P, P)]

    @block.gpsimd
    def _(pool):
        pool.memset(PR_[:, :, E:E + 4], -5.0).then_inc(ready, 1)

        def split_lo(idx, slot, width=4 * P):
            pool.wait_ge(w_hi, idx * 2 + 2)
            for half in range(2):
                h, lo = (half, 0) if width == 4 * P else (0, half * width)
                where = (slice(None), h, slice(lo, lo + width))
                pool.tensor_tensor(place("lo", idx, slot)[where], raw[:, slot][where],
                                   place("hi", idx, slot)[where].bitcast(F32), ALU.subtract).then_inc(w_lo, 1)
        split_lo(0, 0, 2 * P)
        for idx in range(1, EXPERT + 1):
            split_lo(idx, idx % 2)
        pool.wait_ge(sd_hi, NT)
        pool.wait_ge(sd_lo, NT)
        pool.memset(mixed, 0.0).then_inc(ready, 1)
        pool.wait_ge(ready, 2)

        def add_up(e, i):
            for t in range(NG):
                pool.wait_ge(basis_done, e * NG + t + 1)
                dst = mixed[:, i, t * GT:(t + 1) * GT]
                pool.tensor_tensor(dst, dst, BS[:, t % 2, :], ALU.add).then_inc(acc_done, 1)

        def experts(k):
            for i in range(HALF):
                split_lo(k * HALF + EXPERT + 1 + i, (EXPERT + 1 + i) % 2)
                add_up(k * HALF + i, i)

        with pool.Fori(0, KB - 1) as k:
            experts(k)
        experts(KB - 1)

    @block.scalar
    def _(act):
        def split_hi(idx, slot, used=None, width=4 * P):
            act.wait_ge(raw_in[slot], (idx - slot) * 16 + 32)
            if used:
                act.wait_ge(*used)
            for half in range(2):
                h, lo = (half, 0) if width == 4 * P else (0, half * width)
                where = (slice(None), h, slice(lo, lo + width))
                act.activation(place("hi", idx, slot)[where], raw[:, slot][where], ACT.Copy).then_inc(w_hi, 1)

        act.wait_ge(ve_done, 1)
        act.activation(ln["root1"][:], ln["var_eps1"][:], ACT.Sqrt).then_inc(root_done, 1)
        act.wait_ge(consts_in, 48)
        act.activation(col["tanh_gate_f"][:], col["gate_f"][:], ACT.Tanh).then_inc(tg_done, 1)
        split_hi(0, 0, width=2 * P)
        split_hi(1, 1)
        with act.Fori(0, NT // 2) as p:
            for s in range(2):
                act.wait_ge(xn_t, p * 2 + s + 1)
                act.activation(at_tile(XT["hi"], p * 2 + s), PT[:, s, :].rearrange("p (c n) -> p c n", c=HC),
                               ACT.Copy).then_inc(xT_hi, 1)
        for q in range(NG):
            act.wait_ge(router_mm, q + 1)
            if q >= 2:
                act.wait_ge(logits_t, q - 1)
            act.activation(logitsT[:, q % 2, :], PG[:, q % 2, :], ACT.Copy).then_inc(logits_out, 1)

        def silu(n, t):
            q = n * NG + t
            act.wait_ge(gate_mm, q + 1)
            if not isinstance(q, int) or q >= 2:
                act.wait_ge(prod_done, q - 1)
            act.activation(SG[:, t % 2, :], PG[:, t % 2, :], ACT.Silu).then_inc(silu_done, 1)

        for n in range(NS):
            for t in range(NG):
                if n == 0 and t == 0:
                    act.wait_ge(logits_t, NG)
                silu(n, t)
                if t == 1 and n < NS - 1:
                    split_hi(SHARED + n + 1, (SHARED + n + 1) % 2,
                             (router_mm, NG) if n == 0 else (up_mm, n * NG))
                if n == NS - 1 and t < 2:
                    split_hi(SDOWN + t, (SDOWN + t) % 2)
                if n == NS - 1 and t == 2:
                    split_hi(EXPERT, EXPERT % 2, (up_mm, (NS - 1) * NG))
                if n == 0 and t == NG - 1:
                    act.wait_ge(shifted, 1)
                    act.activation(PR_[:, :, 0:E], PR_[:, :, 0:E], ACT.Exp).then_inc(exp_done, 1)
        for q in range(NG):
            act.wait_ge(coeff_t, q + 1)
            act.activation(coeffT[:, q * GT:(q + 1) * GT], PT[:, q % 2, :], ACT.Copy).then_inc(coeff_out, 1)

        def split_rows(src, chunks, done, mm, t, s):
            if not isinstance(t, int) or t >= 2:
                act.wait_ge(mm, t - 1)
            act.activation(DL["hi"][:, s, 0:chunks, :], at_tile(src, t), ACT.Copy).then_inc(done, 1)

        def split_all(src, chunks, done, mm, rows, before):
            act.wait_ge(rows, before + 1)
            for t in range(4):
                split_rows(src, chunks, done, mm, t, t % 2)
            with act.Fori(1, NG) as q:
                act.wait_ge(rows, q + (before + 1))
                for t in range(4):
                    split_rows(src, chunks, done, mm, q * 4 + t, t % 2)

        split_all(hT, 4, sd_hi, sd_mm, prod_done, (NS - 1) * NG)
        def c_out(k, t):
            act.wait_ge(cb_mm, k * NG + t + 1)
            if not isinstance(k, int) or k >= 1:
                act.wait_ge(basis_done, (k - 1) * HALF * NG + (HALF - 1) * NG + t + 1)
            act.activation(cB[:, t * GT:(t + 1) * GT], PT[:, t % 2, :], ACT.Copy).then_inc(cb_out, 1)

        act.wait_ge(sd_hi, NT)
        act.wait_ge(sd_lo, NT)
        for t in range(NG):
            c_out(0, t)

        def experts(k, last):
            for i in range(HALF):
                for t in range(NG):
                    silu(k * HALF + NS + i, t)
                    if t == 1:
                        if last and i == HALF - 1:
                            split_hi(DOWN, DOWN % 2, (sd_mm, NT))
                        else:
                            split_hi(k * HALF + EXPERT + i + 1, (EXPERT + i + 1) % 2,
                                     (up_mm, (k * HALF + NS + i) * NG))
                    if i == HALF - 1 and not last:
                        c_out(k + 1, t)
        with act.Fori(0, KB - 1) as k:
            experts(k, False)
        experts(KB - 1, True)
        split_all(mixed, 2, d_hi, d_mm, acc_done, (NE - 1) * NG)

    @block.vector
    def _(dve):
        count = [0]

        def link(ins):
            count[0] += 1
            ins.then_inc(chain, 1)
            dve.wait_ge(chain, count[0])

        dve.tensor_scalar(ln["var_eps1"][:], mv[:, :, 1], LN_EPS, None, ALU.add).then_inc(ve_done, 1)
        dve.wait_ge(root_done, 1)
        newton_rsqrt(dve, chain, count, ln["var_eps1"][:], ln["root1"][:], ln["rstd1"][:], ln["tmp1"][:])

        def normalise(t, s):
            one = bass.ds(t, 1)
            dve.tensor_scalar(xn[:, s, :], X[:, one, :].rearrange("p o d -> p (o d)"), mv[:, one, 0],
                              ln["rstd1"][:, one], ALU.subtract, ALU.mult).then_inc(xn_ready, 1)

        def turned_low(t, s):
            dve.wait_ge(xT_hi, t + 1)
            dve.tensor_tensor(at_tile(XT["lo"], t), PT[:, s, :].rearrange("p (c n) -> p c n", c=HC),
                              at_tile(XT["hi"], t).bitcast(F32), ALU.subtract).then_inc(xT_lo, 1)

        for s in range(2):
            normalise(s, s)
        with dve.Fori(0, NT // 2 - 1) as p:
            for s in range(2):
                dve.wait_ge(xn_t, p * 2 + s + 1)
                normalise(p * 2 + s + 2, s)
                turned_low(p * 2 + s, s)
        for s in range(2):
            turned_low(NT - 2 + s, s)
        dve.wait_ge(consts_in, 48)
        link(dve.tensor_tensor(amp[:], amp[:], amp[:], ALU.mult))
        link(dve.tensor_tensor(amp2[:], amp[:, :, 0], amp[:, :, 1], ALU.add))
        link(dve.tensor_reduce(col["mix_sum"][:], amp2[:], AX.X, ALU.add))
        link(dve.tensor_scalar(col["mix_sum"][:], col["mix_sum"][:], FFN_EPS, None, ALU.add))
        link(dve.reciprocal(col["mix_sum"][:], col["mix_sum"][:]))
        link(dve.tensor_scalar(mix[:], amp2[:], col["mix_sum"][:, 0:1], escale[:, 0:1], ALU.mult, ALU.mult))
        dve.wait_ge(ready, 1)
        for q in range(NG):
            dve.wait_ge(logits_t, q + 1)
            dve.tensor_copy(PR_[:, q * 4:(q + 1) * 4, 0:E], PT[:, q % 2, :].rearrange("p (t e) -> p t e", e=E)
                            ).then_inc(logits_in, 1)

        def times(n, t, dst):
            q = n * NG + t
            dve.wait_ge(silu_done, q + 1)
            dve.wait_ge(up_mm, q + 1)
            return dve.tensor_tensor(dst, PU[:, t % 2, :], SG[:, t % 2, :], ALU.mult).then_inc(prod_done, 1)

        probs = PR_[:, :, 0:E]

        def over(v):
            return v.unsqueeze(2).broadcast_to([P, NT, E])

        def top_experts(step):
            w = per_tile
            if step == 0:
                dve.wait_ge(logits_in, NG)
                link(dve.tensor_reduce(w["row_max"][:], probs, AX.X, ALU.max))
            elif step == 1:
                dve.tensor_tensor(probs, probs, over(w["row_max"][:]), ALU.subtract).then_inc(shifted, 1)
            elif step == 4:
                dve.wait_ge(exp_done, 1)
                link(dve.tensor_reduce(w["row_sum"][:], probs, AX.X, ALU.add))
                link(dve.reciprocal(w["row_inv"][:], w["row_sum"][:]))
            elif step == 5:
                link(dve.tensor_tensor(probs, probs, over(w["row_inv"][:]), ALU.mult))
            elif step in (6, 7):
                for t in range((step - 6) * 8, (step - 5) * 8):
                    ins = dve.max(top8[:, t, :], PR_[:, t, 0:E])
                link(ins)
            elif step == 8:
                link(dve.tensor_reduce(w["top_sum"][:], top8[:, :, 0:TOPK], AX.X, ALU.add))
                link(dve.tensor_scalar(w["top_sum"][:], w["top_sum"][:], FFN_EPS, None, ALU.add))
                link(dve.reciprocal(w["top_inv"][:], w["top_sum"][:]))
                link(dve.memset(top8[:, :, TOPK:8], -5.0))
            elif step in (9, 10):
                for t in range((step - 9) * 8, (step - 8) * 8):
                    ins = dve.match_replace(probs_left[:, t, :], top8[:, t, :], PR_[:, t, :], 0.0)
                link(ins)
            elif step == 11:
                link(dve.tensor_tensor(probs, probs, probs_left[:, :, 0:E], ALU.subtract))
            elif step == 12:
                dve.tensor_tensor(probs, probs, over(w["top_inv"][:]), ALU.mult).then_inc(coeff_done, 1)

        for n in range(NS):
            for t in range(NG):
                times(n, t, hT[:, n, t * GT:(t + 1) * GT])
                top_experts(n * NG + t)
        dve.wait_ge(tg_done, 1)

        def rest_rows(src, chunks, hi, lo, t, s):
            dve.wait_ge(hi, t + 1)
            dve.tensor_tensor(DL["lo"][:, s, 0:chunks, :], at_tile(src, t), DL["hi"][:, s, 0:chunks, :].bitcast(F32),
                              ALU.subtract).then_inc(lo, 1)

        def add_rows(mm, done, t, s):
            row = X[:, bass.ds(t, 1), :].rearrange("p o d -> p (o d)")
            dve.wait_ge(mm, t + 1)
            dve.scalar_tensor_tensor(out=row, in0=PT[:, s, :], scalar=col["tanh_gate_f"][:, 0:1], in1=row,
                                     op0=ALU.mult, op1=ALU.add).then_inc(done, 1)

        def down(src, chunks, hi, lo, mm, done):
            for s in range(2):
                rest_rows(src, chunks, hi, lo, s, s)
            with dve.Fori(1, NT // 2) as p:
                for s in range(2):
                    add_rows(mm, done, p * 2 + s - 2, s)
                    rest_rows(src, chunks, hi, lo, p * 2 + s, s)
            for s in range(2):
                add_rows(mm, done, NT - 2 + s, s)

        down(hT, 4, sd_hi, sd_lo, sd_mm, sd_out)

        def mix_column(k):
            if not isinstance(k, int) or k >= 1:
                dve.wait_ge(cb_mm, k * NG)
            dve.tensor_copy(MR[:], mix[:, bass.ds(k, 1)].broadcast_to([P, P])).then_inc(mr_ready, 1)

        mix_column(0)

        def experts(k, last):
            for i in range(HALF):
                for t in range(NG):
                    e = k * HALF + i
                    q = e * NG + t
                    if not isinstance(q, int) or q >= 2:
                        dve.wait_ge(acc_done, q - 1)
                    times(e + NS, t, BS[:, t % 2, :])
                    if i == 0:
                        dve.wait_ge(cb_out, k * NG + t + 1)
                    dve.wait_ge(prod_done, (e + NS) * NG + t + 1)
                    dve.tensor_tensor(BS[:, t % 2, :], BS[:, t % 2, :], cB[:, t * GT:(t + 1) * GT],
                                      ALU.mult).then_inc(basis_done, 1)
                if i == 0 and not last:
                    mix_column(k + 1)
        experts(0, False)
        with dve.Fori(1, KB - 1) as k:
            experts(k, False)
        experts(KB - 1, True)
        down(mixed, 2, d_hi, d_lo, d_mm, d_out)

    @block.tensor
    def _(pe):
        def turn_rows(t, s):
            pe.wait_ge(xn_ready, t + 1)
            if not isinstance(t, int):
                pe.wait_ge(xT_lo, t - 1)
            for c in range(HC):
                ins = pe.transpose(PT[:, s, c * P:(c + 1) * P], xn[:, s, c * P:(c + 1) * P], ident[:])
            ins.then_inc(xn_t, 1)

        for s in range(2):
            turn_rows(s, s)
        with pe.Fori(1, NT // 2) as p:
            for s in range(2):
                turn_rows(p * 2 + s, s)

        def proj(out, stat, mov, chunks):
            n = [(c, s, m) for c in range(chunks) for s, m in PASSES]
            for j, (c, s, m) in enumerate(n):
                ins = pe.matmul(out, stat(s, c), mov(m, c), start=j == 0, stop=j == len(n) - 1)
            return ins

        def tokens(t):
            return lambda h, c: XT[h][:, c, t * GT:(t + 1) * GT]

        def weights(slot, half):
            return lambda h, c: WB[h][:, slot, half, c * P:(c + 1) * P]

        pe.wait_ge(xT_lo, NT)
        pe.wait_ge(w_lo, 2)

        def turn_logits(q):
            pe.wait_ge(logits_out, q + 1)
            if q >= 2:
                pe.wait_ge(logits_in, q - 1)
            for j in range(4):
                ins = pe.transpose(PT[:, q % 2, j * P:(j + 1) * P], logitsT[:, q % 2, j * P:(j + 1) * P], ident[:])
            ins.then_inc(logits_t, 1)

        for q in range(NG):
            if q >= 2:
                pe.wait_ge(logits_out, q - 1)
            ins = proj(PG[:, q % 2, :], weights(0, 0), tokens(q), HC).then_inc(router_mm, 1)
            if q >= 1:
                turn_logits(q - 1)
        turn_logits(NG - 1)

        def gate_up(n, slot, t):
            q = n * NG + t
            if not isinstance(q, int) or q >= 2:
                pe.wait_ge(silu_done, q - 1)
            proj(PG[:, t % 2, :], weights(slot, 0), tokens(t), HC).then_inc(gate_mm, 1)
            if not isinstance(q, int) or q >= 2:
                pe.wait_ge(prod_done, q - 1)
            proj(PU[:, t % 2, :], weights(slot, 1), tokens(t), HC).then_inc(up_mm, 1)

        for n in range(NS):
            pe.wait_ge(w_lo, 2 * (SHARED + n) + 2)
            for t in range(NG):
                gate_up(n, (SHARED + n) % 2, t)

        def down(chunks, weight, lo, mm, done, t, s):
            pe.wait_ge(lo, t + 1)
            if not isinstance(t, int) or t >= 2:
                pe.wait_ge(done, t - 1)
            return proj(PT[:, s, :], lambda h, c: DL[h][:, s, c, :], weight, chunks).then_inc(mm, 1)

        def down_w(h, c):
            return WD[h][:, c, :]

        pe.wait_ge(coeff_done, 1)
        for q in range(NG):
            if q >= 2:
                pe.wait_ge(coeff_out, q - 1)
            for j in range(4):
                ins = pe.transpose(PT[:, q % 2, j * P:(j + 1) * P], PR_[:, q * 4 + j, 0:E], ident[:])
            ins.then_inc(coeff_t, 1)
        pe.wait_ge(coeff_out, NG)
        pe.wait_ge(w_lo, 2 * SDOWN + 4)
        for s in range(2):
            down(4, down_w, sd_lo, sd_mm, sd_out, s, s)
        with pe.Fori(1, NT // 2) as p:
            for s in range(2):
                down(4, down_w, sd_lo, sd_mm, sd_out, p * 2 + s, s)
        def c_rows(k, t):
            if t == 0:
                pe.wait_ge(mr_ready, k + 1)
            if not isinstance(k, int) or k * NG + t >= 2:
                pe.wait_ge(cb_out, k * NG + t - 1)
            pe.matmul(PT[:, t % 2, :], MR[:], coeffT[:, t * GT:(t + 1) * GT], start=True, stop=True).then_inc(cb_mm, 1)

        pe.wait_ge(sd_out, NT)
        for t in range(NG):
            c_rows(0, t)

        def experts(k, last):
            for i in range(HALF):
                pe.wait_ge(w_lo, (k * HALF + EXPERT + i) * 2 + 2)
                for t in range(NG):
                    gate_up(k * HALF + NS + i, (EXPERT + i) % 2, t)
                    if i == HALF - 1 and not last:
                        c_rows(k + 1, t)
        with pe.Fori(0, KB - 1) as k:
            experts(k, False)
        experts(KB - 1, True)

        pe.wait_ge(w_lo, 2 * DOWN + 2)
        pe.wait_ge(cb_out, KB * NG)
        for s in range(2):
            down(2, down_w, d_lo, d_mm, d_out, s, s)
        with pe.Fori(1, NT // 2) as p:
            for s in range(2):
                down(2, down_w, d_lo, d_mm, d_out, p * 2 + s, s)


def build(nc, a, out):
    with ExitStack() as whole:
        X = whole.enter_context(nc.sbuf_tensor("x_rows", [P, NT, HID], F32))
        ident = whole.enter_context(nc.sbuf_tensor("ident", [P, P], F32))
        x1_mv = whole.enter_context(nc.sbuf_tensor("x1_mean_var", [P, NT, 2], F32))
        with ExitStack() as ctx:
            build_attention(nc, ctx, a, X, ident, x1_mv)
        with ExitStack() as ctx:
            build_ffn(nc, ctx, a, X, ident, x1_mv, out)


def constants():
    p = np.arange(P)
    key = (np.arange(4 * W) // (2 * W) - 1) * W + np.arange(4 * W) % W
    rel = key[None, :] - (p % W)[:, None]
    inside = (rel <= 0) & (rel > -W)
    slope = np.power(np.float32(2.0), np.float32(-8.0) * np.arange(H, dtype=np.float32) / np.float32(H))
    pair = np.arange(2 * HK)
    heads = (pair // 2 * G + pair % 2 * 2)[None, :] + (p // W)[:, None]
    return {
        "identity": np.eye(P, dtype=np.float32),
        "slopes": (slope[heads] * np.float32(D ** 0.5)).astype(np.float32),
        "rel_pen": np.stack([rel, np.where(inside, 0.0, MASKED)], 1).astype(np.float32),
    }


def kernel(**inputs):
    import concourse.bacc as bacc
    from concourse.bass_utils import run_bass_kernel_spmd

    nc = bacc.Bacc("TRN2", target_bir_lowering=False, num_devices=1)
    arrays, aps = {}, {}
    for name, v in {**inputs, **constants()}.items():
        v = np.ascontiguousarray(v)
        arrays[f"in_{name}"] = v
        aps[name] = nc.dram_tensor(f"in_{name}", v.shape, mybir.dt.from_np(v.dtype), kind="ExternalInput").ap()
    out = nc.dram_tensor("out", (B, T, HID), F32, kind="ExternalOutput").ap()
    build(nc, aps, out)
    return run_bass_kernel_spmd(nc, [arrays], core_ids=[0]).results[0]["out"]
```
